# Optimizing a Trainium2 kernel written in Bass

```python
import numpy as np
import jax
import jax.numpy as jnp

def _softmax(x, axis=-1):
    return jax.nn.softmax(x, axis=axis)

def _gelu(x):
    return jax.nn.gelu(x, approximate=True)

def _silu(x):
    return jax.nn.silu(x)

def _sigmoid(x):
    return jax.nn.sigmoid(x)

def _layernorm(x, axis=-1, eps=1e-05):
    m = jnp.mean(x, axis=axis, keepdims=True)
    v = jnp.var(x, axis=axis, keepdims=True)
    return (x - m) / jnp.sqrt(v + eps)

def _scatter_add(tgt, idx, src, axis=0):
    return tgt.at[idx].add(src)

def _segment_sum(src, seg, n):
    return jax.ops.segment_sum(src, seg, n)
kernel_name = 'mk_flamingo_gated_d1_seqx_r4_055dad'

def setup_inputs(seed: int=0):
    np.random.seed(seed)
    _w = jnp.asarray

    def _rec_inputs():
        import jax
        import jax.numpy as jnp
        _rk = jax.random.key(seed)
        x = -0.0002928 + 1 * jax.random.normal(jax.random.fold_in(_rk, 1), (8, 512, 256), jnp.float32)
        _lenS = 512 - jax.random.randint(jax.random.fold_in(_rk, 7), (8,), 0, max(1, 512 // 4) + 1, jnp.int32)
        _lenS2 = 1024 - jax.random.randint(jax.random.fold_in(_rk, 8), (8,), 0, max(1, 1024 // 4) + 1, jnp.int32)
        _ctx_1024P = jax.random.normal(jax.random.fold_in(_rk, 11), (8, 16, 256), jnp.float32)
        _ctx_1024c = jax.random.dirichlet(jax.random.fold_in(_rk, 511), 0.3 * jnp.ones((16,), jnp.float32), (8, 1024))
        _ctx_1024t = jnp.einsum('bsk,bkd->bsd', _ctx_1024c, _ctx_1024P)
        _ctx_1024t = _ctx_1024t * jax.lax.rsqrt(jnp.mean(jnp.square(_ctx_1024t)) + 1e-12) * 0.953939
        ctx_1024 = -1.52775e-05 + 0.999936 * (_ctx_1024t + 0.3 * jax.random.normal(jax.random.fold_in(_rk, 611), (8, 1024, 256), jnp.float32))
        _g = jax.random.normal(jax.random.fold_in(_rk, 9001), (2, 1), jnp.float32)
        _g = jnp.sign(_g) * jnp.maximum(jnp.abs(_g), 1.0) + (_g == 0) * 1.0
        g_xattn = _g[0]
        g_ffn = _g[1]
        return (x, ctx_1024, g_xattn, g_ffn)
    x, ctx_1024, g_xattn, g_ffn = _rec_inputs()

    def _L0_xattn_setup():
        import jax, jax.numpy as jnp
        import numpy as np
        DIM = 256
        NUM_HEADS = 8
        HEAD_DIM = 64
        INNER = NUM_HEADS * HEAD_DIM
        key = jax.random.key(seed)
        ks = jax.random.split(key, 7)
        B, N, M = (8, 128, 1024)
        x = jax.random.normal(ks[0], (B, N, DIM), dtype=jnp.float32)
        context = jax.random.normal(ks[1], (B, M, DIM), dtype=jnp.float32)
        s_in = 1.0 / np.sqrt(DIM)
        s_inner = 1.0 / np.sqrt(INNER)
        Wq = jax.random.normal(ks[2], (DIM, INNER), dtype=jnp.float32) * s_in
        Wk = jax.random.normal(ks[3], (DIM, INNER), dtype=jnp.float32) * s_in
        Wv = jax.random.normal(ks[4], (DIM, INNER), dtype=jnp.float32) * s_in
        Wo = jax.random.normal(ks[5], (INNER, DIM), dtype=jnp.float32) * s_inner
        bo = jax.random.normal(ks[6], (DIM,), dtype=jnp.float32) * 0.01
        return {'x': x, 'context': context, 'Wq': Wq, 'Wk': Wk, 'Wv': Wv, 'Wo': Wo, 'bo': bo}
    _L0_xattn_all = _L0_xattn_setup()
    _L0_xattn_in = {k: v for k, v in _L0_xattn_all.items() if k in ('Wq', 'Wk', 'Wv', 'Wo', 'bo')}
    del _L0_xattn_all

    def _L0_ffn_setup():
        import jax, jax.numpy as jnp
        import numpy as np
        import math
        DMODEL = 256
        DFF = 1024
        NUM_EXPERTS = 8
        TOPK = 2
        CAP_FACTOR = 1.25
        EPS = 1.1920929e-07

        def _trunc_normal(key, shape, fan_in, scale=1.0):
            std = scale * (1.0 / fan_in) ** 0.5
            return jax.random.truncated_normal(key, -2.0, 2.0, shape, jnp.float32) * std
        key = jax.random.key(seed)
        ks = jax.random.split(key, 5)
        return {'x': jax.random.normal(ks[0], (2, 512, DMODEL), jnp.float32), 'router_weight': _trunc_normal(ks[1], (NUM_EXPERTS, DMODEL), DMODEL), 'ff_pre_act_weight': _trunc_normal(ks[2], (NUM_EXPERTS, DFF, DMODEL), DMODEL), 'gate_weight': _trunc_normal(ks[3], (NUM_EXPERTS, DFF, DMODEL), DMODEL), 'ff_post_act_weight': _trunc_normal(ks[4], (NUM_EXPERTS, DMODEL, DFF), DFF)}
    _L0_ffn_all = _L0_ffn_setup()
    _L0_ffn_in = {k: v for k, v in _L0_ffn_all.items() if k in ('router_weight', 'ff_pre_act_weight', 'gate_weight', 'ff_post_act_weight')}
    del _L0_ffn_all
    return {'x': x, 'ctx_1024': ctx_1024, 'g_xattn': g_xattn, 'g_ffn': g_ffn, 'L0_xattn_Wq': _L0_xattn_in['Wq'], 'L0_xattn_Wk': _L0_xattn_in['Wk'], 'L0_xattn_Wv': _L0_xattn_in['Wv'], 'L0_xattn_Wo': _L0_xattn_in['Wo'], 'L0_xattn_bo': _L0_xattn_in['bo'], 'L0_ffn_router_weight': _L0_ffn_in['router_weight'], 'L0_ffn_ff_pre_act_weight': _L0_ffn_in['ff_pre_act_weight'], 'L0_ffn_gate_weight': _L0_ffn_in['gate_weight'], 'L0_ffn_ff_post_act_weight': _L0_ffn_in['ff_post_act_weight']}

def reference(x, ctx_1024, g_xattn, g_ffn, L0_xattn_Wq, L0_xattn_Wk, L0_xattn_Wv, L0_xattn_Wo, L0_xattn_bo, L0_ffn_router_weight, L0_ffn_ff_pre_act_weight, L0_ffn_gate_weight, L0_ffn_ff_post_act_weight):
    import jax
    import jax.numpy as jnp

    def _L0_xattn_ref(x, context, Wq, Wk, Wv, Wo, bo):
        import jax, jax.numpy as jnp
        import numpy as np
        DIM = 256
        NUM_HEADS = 8
        HEAD_DIM = 64
        INNER = NUM_HEADS * HEAD_DIM
        B, N, _ = x.shape
        M = context.shape[1]
        scale = HEAD_DIM ** (-0.5)
        q = (x @ Wq).reshape(B, N, NUM_HEADS, HEAD_DIM).transpose(0, 2, 1, 3)
        k = (context @ Wk).reshape(B, M, NUM_HEADS, HEAD_DIM).transpose(0, 2, 1, 3)
        v = (context @ Wv).reshape(B, M, NUM_HEADS, HEAD_DIM).transpose(0, 2, 1, 3)
        attn = jax.nn.softmax(jnp.einsum('bhnd,bhmd->bhnm', q, k) * scale, axis=-1)
        out = jnp.einsum('bhnm,bhmd->bhnd', attn, v)
        out = out.transpose(0, 2, 1, 3).reshape(B, N, INNER)
        return out @ Wo + bo

    def _L0_ffn_ref(x, router_weight, ff_pre_act_weight, gate_weight, ff_post_act_weight):
        import jax, jax.numpy as jnp
        import numpy as np
        import math
        DMODEL = 256
        DFF = 1024
        NUM_EXPERTS = 8
        TOPK = 2
        CAP_FACTOR = 1.25
        EPS = 1.1920929e-07

        def _trunc_normal(key, shape, fan_in, scale=1.0):
            std = scale * (1.0 / fan_in) ** 0.5
            return jax.random.truncated_normal(key, -2.0, 2.0, shape, jnp.float32) * std
        orig_shape = x.shape
        h = x.reshape(-1, DMODEL)
        T = h.shape[0]
        logits = jnp.einsum('th,eh->te', h, router_weight)
        probs = jax.nn.softmax(logits.astype(jnp.float32), axis=-1)
        topk_probs, selected = jax.lax.top_k(probs, TOPK)
        topk_probs = topk_probs / jnp.maximum(topk_probs.sum(-1, keepdims=True), EPS)
        flat_tokens = jnp.repeat(jnp.arange(T), TOPK)
        flat_experts = selected.reshape(-1)
        flat_weights = topk_probs.reshape(-1)
        A = T * TOPK
        capacity = max(1, math.ceil(CAP_FACTOR * A / NUM_EXPERTS))
        weight_order = jnp.argsort(-flat_weights, stable=True)
        grouped_order = jnp.argsort(flat_experts[weight_order], stable=True)
        sort_order = weight_order[grouped_order]
        se = flat_experts[sort_order]
        st = flat_tokens[sort_order]
        sw = flat_weights[sort_order]
        counts = jnp.bincount(se, length=NUM_EXPERTS)
        offsets = jnp.cumsum(counts) - counts
        slot = jnp.arange(A) - offsets[se]
        keep = slot < capacity
        sw = jnp.where(keep, sw, 0.0)
        token_wsum = jnp.zeros(T, jnp.float32).at[st].add(sw)
        kept_w = sw / jnp.maximum(token_wsum[st], EPS)
        FC = NUM_EXPERTS * capacity
        dispatch = jnp.where(keep, se * capacity + slot, FC)
        expert_inputs = jnp.zeros((FC + 1, DMODEL), x.dtype).at[dispatch].set(h[st])
        expert_inputs = expert_inputs[:FC].reshape(NUM_EXPERTS, capacity, DMODEL)
        pre = jnp.einsum('ech,edh->ecd', expert_inputs, ff_pre_act_weight)
        gate = jnp.einsum('ech,edh->ecd', expert_inputs, gate_weight)
        expert_out = jnp.einsum('ecd,ehd->ech', pre * jax.nn.silu(gate), ff_post_act_weight)
        eo_flat = jnp.concatenate([expert_out.reshape(FC, DMODEL), jnp.zeros((1, DMODEL), x.dtype)], axis=0)
        updates = eo_flat[dispatch] * kept_w.astype(x.dtype)[:, None]
        out = jnp.zeros((T, DMODEL), x.dtype).at[st].add(updates)
        return out.reshape(orig_shape)
    x = x + jnp.tanh(g_xattn[0]) * _L0_xattn_ref(_layernorm(x, axis=-1), ctx_1024, L0_xattn_Wq, L0_xattn_Wk, L0_xattn_Wv, L0_xattn_Wo, L0_xattn_bo)
    x = x + jnp.tanh(g_ffn[0]) * _L0_ffn_ref(_layernorm(x, axis=-1), L0_ffn_router_weight, L0_ffn_ff_pre_act_weight, L0_ffn_gate_weight, L0_ffn_ff_post_act_weight)
    return x

_drawn_inputs = setup_inputs


def setup_inputs(seed=0):
    import zlib

    import numpy as np

    out = dict(_drawn_inputs(seed))
    spreads = {}
    factors = {'L0_xattn_bo': 3.243}
    for name, (base, spread) in spreads.items():
        noise = np.random.default_rng([zlib.crc32(name.encode()), seed]).standard_normal(out[name].shape)
        drawn = base * np.exp(spread * noise) if base else spread * noise
        out[name] = jnp.asarray(drawn.astype(out[name].dtype))
    for name, factor in factors.items():
        out[name] = (out[name] * factor).astype(out[name].dtype)
    return out
```

```python
from contextlib import ExitStack

import concourse.bass as bass
from concourse import mybir
from concourse.bass import ds

F32 = mybir.dt.float32
F32R = mybir.dt.float32r
BF16 = mybir.dt.bfloat16
I32 = mybir.dt.int32
U32 = mybir.dt.uint32
ALU = mybir.AluOpType
ACT = mybir.ActivationFunctionType
AX = mybir.AxisListType

P = 128
B, N, D = 8, 512, 256
M = 1024
H, DH = 8, 64
INNER = H * DH
T = B * N
KC = D // P
QT = N // P
KT = M // P
UNITS = H * QT
PAIRS = H // 2
SCALE = DH ** -0.5
LN_EPS = 1e-5

E = 8
GROUPS = P // E
GT = T // GROUPS
FF = 1024
FC = FF // P
EPS = 1.1920929e-07
CAPACITY = (T * 2 * 5 + 4 * E - 1) // (4 * E)
WEIGHT_BITS = 30
CHUNK = 256
ST = CHUNK // P
MOST_CHUNKS = 2 * T // CHUNK + 2 * E
PAD = 2 * CHUNK
ROWS = T + PAD
RW = D + 4

JOBS = {
    0: [("q", 1, 0)], 1: [("k", 1, 0)], 2: [("k", 1, 1)], 3: [("w", 1, 0)], 5: [("w", 1, 1)],
    6: [("v", 1, 0)], 7: [("v", 1, 1)], 8: [("q", 2, 0)], 9: [("h", 0, 0)], 10: [("k", 2, 0)],
    11: [("h", 1, 0)], 12: [("k", 2, 1)], 13: [("l", 0, 0)], 14: [("v", 1, 2)], 15: [("v", 1, 3)],
    16: [("q", 3, 0)], 17: [("k", 3, 0), ("r", 0, 0)], 18: [("k", 3, 1)], 19: [("w", 0, 0)],
    20: [("x", 0, 0)], 21: [("w", 0, 1)], 22: [("x", 1, 0)], 24: [("v", 0, 0)], 25: [("v", 0, 1)],
    26: [("v", 0, 2)], 27: [("q", 0, 0)], 28: [("v", 0, 3)], 29: [("k", 0, 0)], 30: [("k", 0, 1)],
}
GATE_STEPS = 23
RANK_STEPS = 5
CONSTS = 15
END_STEPS = 18


class Body:

    def __init__(self, b, prev, own, nxt, offset, before):
        self.b, self.prev, self.own, self.nxt, self.before = b, prev, own, nxt, before
        self.offset = offset
        self.steps, place = [], offset
        for u in range(UNITS if own or nxt else END_STEPS):
            mine = []
            if u % 2 == 0 and (prev if u < 4 else own):
                mine.append(("o", ((u - 4) % UNITS) // 2, 0))
            for job in JOBS.get(u, []):
                if job[0] in "hlr" or job[:2] == ("w", 1):
                    wanted = prev
                elif job[0] in "xqkv" and u >= 20:
                    wanted = nxt
                else:
                    wanted = own
                if wanted:
                    mine.append(job)
            self.steps.append([(job, place + i) for i, job in enumerate(mine)])
            place += len(mine)
        self.end = place
        self.where = {job: c for step in self.steps for job, c in step}

    def of(self, b):
        return Body(b, self.prev, self.own, self.nxt, self.offset, self.before)

    def place(self, job):
        if job[0] != "x" and job[1] > 0:
            return self.where[job]
        return self.before.where[job] - RING


RING = Body(1, True, True, True, 0, None).end
START = Body(-1, False, False, True, RING, None)
FIRST = Body(0, False, True, True, START.end - RING, START)
MIDDLE = Body(1, True, True, True, FIRST.end - RING, None)
MIDDLE.before = MIDDLE
LAST = Body(B - 1, True, True, False, MIDDLE.end - RING, MIDDLE)
END = Body(B, True, False, False, LAST.end - RING, LAST)
assert RING % 2 == 0 and MIDDLE.end - RING == FIRST.end - RING


def at(b, per_batch, n):
    return b * per_batch + n


def until(eng, sem, value):
    if not isinstance(value, int) or value > 0:
        eng.wait_ge(sem, value)


def build(nc, x, ctx_t, g_attn, g_ffn, wq, wk, wv, wo, bo, rw_t, w1_t, wg_t, w2_t, out):
    lists = nc.dram_tensor("lists", (E * ROWS, RW), F32, kind="Internal").ap()
    weights_of = nc.dram_tensor("weights_of", (E * ROWS, 1), F32, kind="Internal").ap()

    with ExitStack() as ctx:
        def sem(name):
            return ctx.enter_context(nc.semaphore(name))

        def tile(where, name, shape, dt=F32):
            return where.enter_context(nc.sbuf_tensor(name, shape, dt))

        ident = tile(ctx, "ident", [P, P])
        tanh_g = tile(ctx, "tanh_g", [P, 2])
        assigned = tile(ctx, "assigned", [P, E, T // P])
        list_end = tile(ctx, "list_end", [P, E])
        expert_row = tile(ctx, "expert_row", [P, E])
        same_expert = tile(ctx, "same_expert", [P, P])
        before_it = tile(ctx, "before_it", [P, P])
        same_group = tile(ctx, "same_group", [P, P])

        attn = ExitStack()
        wq_h = tile(attn, "wq_h", [P, KC, INNER], F32R)
        wq_l = tile(attn, "wq_l", [P, KC, INNER], F32R)
        wk_h = tile(attn, "wk_h", [P, KC, INNER], F32R)
        wk_l = tile(attn, "wk_l", [P, KC, INNER], F32R)
        wv_h = tile(attn, "wv_h", [P, KC, INNER], F32R)
        wv_l = tile(attn, "wv_l", [P, KC, INNER], F32R)
        wo_h = tile(attn, "wo_h", [P, H, D], F32R)
        wo_l = tile(attn, "wo_l", [P, H, D], F32R)
        ctx_raw = tile(attn, "ctx_raw", [P, KC, M // 2])
        x_in = tile(attn, "x_in", [P, QT, D])
        h_t = x_in[:, :, :].rearrange("p q (c t) -> p q c t", c=KC)
        x_sum = tile(attn, "x_sum", [P, QT, D])
        rows = tile(attn, "rows", [P, QT, RW])
        bias_o = tile(attn, "bias_o", [P, D])
        rw = tile(attn, "rw", [P, KC, E])
        ctx_h = tile(attn, "ctx_h", [P, KC, M], F32R)
        ctx_l = tile(attn, "ctx_l", [P, KC, M], F32R)
        xt_h = tile(attn, "xt_h", [P, KC, N], F32R)
        xt_l = tile(attn, "xt_l", [P, KC, N], F32R)
        k_st = tile(attn, "k_st", [P, 2, 2, M], F32R)
        q_h = tile(attn, "q_h", [P, 2, 2, N], F32R)
        q_l = tile(attn, "q_l", [P, 2, 2, N], F32R)
        v_hl = tile(attn, "v_hl", [P, KT, H, P], F32R)
        probs = tile(attn, "probs", [P, 2, M])
        pt_h = tile(attn, "pt_h", [P, 2, KT, 2 * P], F32R)
        pt_l = tile(attn, "pt_l", [P, 2, KT, 2 * P], F32R)
        ot_h = tile(attn, "ot_h", [P, H // 2, N], F32R)
        ot_l = tile(attn, "ot_l", [P, H // 2, N], F32R)
        row_max = tile(attn, "row_max", [P, 2])
        neg_max = tile(attn, "neg_max", [P, 2])
        row_sum = tile(attn, "row_sum", [P, 2])
        row_rec = tile(attn, "row_rec", [P, 2])
        earlier = tile(attn, "earlier", [P, P], BF16)
        ones = tile(attn, "ones", [P, P], BF16)
        chosen = tile(attn, "chosen", [P, QT, E], BF16)
        stats = tile(attn, "stats", [P, 2, QT, 6])
        mean_var = tile(attn, "mean_var", [P, 2, QT, 2])
        norm = tile(attn, "norm", [P, 2, 6, QT])
        minus_half = tile(attn, "minus_half", [P, QT])
        rev = tile(attn, "rev", [P, E])
        token = tile(attn, "token", [P, QT])
        gate = tile(attn, "gate", [P, 8, QT, E])
        gate1 = tile(attn, "gate1", [P, 8, QT])
        oh = tile(attn, "oh", [P, 2, QT, E])
        oh_x = tile(attn, "oh_x", [P, 2, QT, E])
        row_f = tile(attn, "row_f", [P, 2, QT])
        list_row = tile(attn, "list_row", [P, 2, QT], U32)
        attn.close()

        moe = ExitStack()
        w_raw = [tile(moe, f"{n}_raw", [P, KC * FF]) for n in ("w1", "wg", "w2")]
        w_h = [[tile(moe, f"{n}_h{i}", [P, KC * FF], F32R) for n in ("w1", "wg", "w2")]
               for i in range(2)]
        w_l = [[tile(moe, f"{n}_l{i}", [P, KC * FF], F32R) for n in ("w1", "wg", "w2")]
               for i in range(2)]
        e_rows = tile(moe, "e_rows", [P, ST, RW])
        et_h = tile(moe, "et_h", [P, KC, CHUNK], F32R)
        et_l = tile(moe, "et_l", [P, KC, CHUNK], F32R)
        silu = tile(moe, "silu", [P, CHUNK])
        act_f = tile(moe, "act_f", [P, 2, CHUNK])
        act_h = tile(moe, "act_h", [P, FC, CHUNK], F32R)
        act_l = tile(moe, "act_l", [P, FC, CHUNK], F32R)
        y = tile(moe, "y", [P, ST, D])
        pad_rows = tile(moe, "pad_rows", [P, PAD // P, RW])
        zeros = tile(moe, "zeros", [P, PAD // P, D])
        y_weight = tile(moe, "y_weight", [P, ST])
        next_token = tile(moe, "next_token", [P, ST])
        y_token = tile(moe, "y_token", [P, ST], U32)
        y_at = tile(moe, "y_at", [P, ST], U32)
        e_base = tile(moe, "e_base", [P, 1])
        by_expert = tile(moe, "by_expert", [P, GT])
        work = tile(moe, "work", [P, 5, GT])
        threshold = tile(moe, "threshold", [P, 1], I32)
        candidate = tile(moe, "candidate", [P, 1], I32)
        raised = tile(moe, "raised", [P, 1], I32)
        bit = tile(moe, "bit", [P, 1], I32)
        bit_f = tile(moe, "bit_f", [P, 1])
        counts = tile(moe, "counts", [P, 4])
        table_f = tile(moe, "table_f", [P, 3, E])
        table = tile(moe, "table", [P, 4, E], I32)
        moe.close()

        banks = ExitStack()
        scores = banks.enter_context(nc.psum_tensor("scores", [P, 2, M], F32))
        turned = banks.enter_context(nc.psum_tensor("turned", [P, 2, N], F32))
        ring = banks.enter_context(nc.psum_tensor("ring", [P, 2, 512], F32))
        banks.close()
        banks = ExitStack()
        ffn1 = banks.enter_context(nc.psum_tensor("ffn1", [P, 4, 2, CHUNK], F32))
        e_turned = banks.enter_context(nc.psum_tensor("e_turned", [P, KC, CHUNK], F32))
        ffn2 = banks.enter_context(nc.psum_tensor("ffn2", [P, ST, 512], F32))
        misc = banks.enter_context(nc.psum_tensor("misc", [P, 512], F32))
        banks.close()

        x_loaded = sem("x_loaded")
        ctx_loaded = sem("ctx_loaded")
        sum_loaded = sem("sum_loaded")
        small_loaded = sem("small_loaded")
        raw_loaded = [sem(f"raw_loaded{i}") for i in range(5)]
        consts = sem("consts")
        waited = sem("waited")
        tanh_done = sem("tanh_done")
        bias_done = sem("bias_done")
        raw_hi = sem("raw_hi")
        weights_split = sem("weights_split")
        ctx_hi = sem("ctx_hi")
        ctx_split = sem("ctx_split")
        scores_done = sem("scores_done")
        max_done = sem("max_done")
        neg_done = sem("neg_done")
        exp_done = sem("exp_done")
        rec_done = sem("rec_done")
        scaled = sem("scaled")
        turned_done = sem("turned_done")
        pt_hi = sem("pt_hi")
        pt_lo = sem("pt_lo")
        filled = sem("filled")
        drained = [sem("drained0"), sem("drained1")]
        hi_done = {k: sem(f"hi_{k}") for k in "qkvox"}
        hi_events = {"q": PAIRS, "k": H, "v": KT, "o": 2 * H, "x": KC}
        ln_seq = [sem("ln1_seq"), sem("ln2_seq")]
        var_done = [sem("var1_done"), sem("var2_done")]
        pow_done = [sem("pow1_done"), sem("pow2_done")]
        scaled_ln = [sem("scaled_ln1"), sem("scaled_ln2")]
        ln_ready = [sem("ln1_ready"), sem("ln2_ready")]
        normed = [sem("normed1"), sem("normed2")]
        biased = sem("biased")
        sum_stored = sem("sum_stored")
        gate_seq = sem("gate_seq")
        gate_exp = sem("gate_exp")
        chosen_done = sem("chosen_done")
        rank_seq = sem("rank_seq")
        list_row_done = sem("list_row_done")
        listed = sem("listed")
        more_done = sem("more_done")
        gathered = sem("gathered")
        search_seq = sem("search_seq")
        search_bits = sem("search_bits")
        counted = sem("counted")
        summed = sem("summed")
        kept = sem("kept")
        wsum_done = sem("wsum_done")
        table_done = sem("table_done")
        fw_done = sem("fw_done")
        fw_stored = sem("fw_stored")
        pads_ready = sem("pads_ready")
        pads_stored = sem("pads_stored")
        w_first = [sem(f"w_first{i}") for i in range(3)]
        w_loaded = [sem(f"w_loaded{i}") for i in range(3)]
        w_hi = sem("w_hi")
        w_split = sem("w_split")
        rows_loaded = sem("rows_loaded")
        e_turned_done = sem("e_turned_done")
        et_hi = sem("et_hi")
        et_lo = sem("et_lo")
        ffn1_done = sem("ffn1_done")
        silu_done = sem("silu_done")
        act_done = sem("act_done")
        act_hi = sem("act_hi")
        act_lo = sem("act_lo")
        ffn2_done = sem("ffn2_done")
        y_done = [sem("y_done0"), sem("y_done1")]
        token_seen = sem("token_seen")
        token_copied = sem("token_copied")
        token_done = sem("token_done")
        base_done = sem("base_done")
        weight_here = sem("weight_here")
        added = sem("added")

        def alone(eng):
            eng.sem_inc(waited, 1)

        def wait_filled(eng, body, c):
            eng.wait_ge(filled, at(body.b, RING, c + 1))

        def wait_drained(eng, body, c):
            until(eng, drained[c % 2], at(body.b, RING // 2, c // 2 + 1))

        def wait_all_drained(eng, body, places):
            for bank in range(2):
                of_bank = [c for c in places if c % 2 == bank]
                if of_bank:
                    wait_drained(eng, body, max(of_bank))

        def batches(eng, run):
            run(START)
            run(FIRST)
            with eng.Fori(1, B - 1) as b:
                run(MIDDLE.of(b))
            run(LAST)
            run(END)

        def wait_hi(eng, kind, b, n):
            eng.wait_ge(hi_done[kind], at(b, hi_events[kind], n + 1))

        def of_batch(body, job, u):
            kind, i, j = job
            b = body.b
            if kind == "o":
                return (b - 1 if u < 4 else b), i
            if u >= 20:
                b = b + 1
            return b, {"q": i, "k": 2 * i + j, "v": 4 * i + j, "x": i}[kind]

        def load_w(eng, i, e, s):
            w = (w1_t, wg_t, w2_t)[i]
            k = w.shape[0] // E
            eng.dma_start(w_raw[i][:, :].rearrange("p (c n) -> p c n", c=k // P),
                          w[ds(e * k, k), :].rearrange("(c p) n -> p c n", p=P))\
                .then_inc(s, 16)

        block = ctx.enter_context(nc.Block())

        @block.sync
        def _(sp):
            def load_x(b, dst, s):
                sp.dma_start(dst[:, :, :], x[ds(b * N, N), :].rearrange("(q p) d -> p q d", p=P))\
                    .then_inc(s, 16)

            def load_ctx(b, half):
                src = ctx_t[ds(b * D, D), half * (M // 2):(half + 1) * (M // 2)]
                sp.dma_start(ctx_raw[:, :, :], src.rearrange("(c p) m -> p c m", p=P))\
                    .then_inc(ctx_loaded, 16)

            def store_sum(b):
                sp.dma_start(out[ds(b * N, N), :].rearrange("(q p) d -> p q d", p=P), x_sum[:, :, :])\
                    .then_inc(sum_stored, 16)

            def start():
                load_x(0, x_in, x_loaded)
                load_ctx(0, 0)
                for i, (w, dst) in enumerate(((wq, probs[:, 0, :]), (wk, probs[:, 1, :]),
                                              (wv, x_sum[:, :, :].rearrange("p q d -> p (q d)")))):
                    sp.dma_start(dst.rearrange("p (c n) -> p c n", c=KC),
                                 w.rearrange("(c p) n -> p c n", p=P)).then_inc(raw_loaded[i], 16)
                sp.dma_start(tanh_g[:, 0:1], g_attn.partition_broadcast(P)).then_inc(small_loaded, 16)
                sp.dma_start(tanh_g[:, 1:2], g_ffn.partition_broadcast(P)).then_inc(small_loaded, 16)
                sp.dma_start(bias_o[:, :], bo.partition_broadcast(P)).then_inc(small_loaded, 16)
                sp.dma_start(rw[:, :, :], rw_t.rearrange("(c p) e -> p c e", p=P))\
                    .then_inc(small_loaded, 16)
                sp.wait_ge(ctx_split, 1)
                load_ctx(0, 1)

            def load_wo():
                for half in range(2):
                    sp.wait_ge(weights_split, 3 + half)
                    for copy_ in range(2):
                        sp.dma_start(x_sum[copy_ * DH:(copy_ + 1) * DH, :, :],
                                     wo[half * (INNER // 2):(half + 1) * (INNER // 2), :]
                                     .rearrange("(h p) d -> p h d", p=DH))\
                            .then_inc(raw_loaded[3 + half], 16)
                sp.wait_ge(weights_split, 5)

            def run(body):
                b = body.b
                if body is START:
                    start()
                    return
                if body.nxt:
                    sp.wait_ge(ctx_split, at(b, 2, 2))
                    alone(sp)
                    load_ctx(b + 1, 0)
                if body.prev:
                    wait_drained(sp, body, body.where[("w", 1, 1)])
                    alone(sp)
                    store_sum(b - 1)
                    sp.wait_ge(sum_stored, at(b, 16, 0))
                    alone(sp)
                    sp.wait_ge(normed[1], at(b, QT, 0))
                    alone(sp)
                else:
                    load_wo()
                if body.own:
                    load_x(b, x_sum, sum_loaded)
                if body.nxt:
                    if body.prev:
                        wait_filled(sp, body, body.where[("l", 0, 0)])
                        alone(sp)
                    else:
                        wait_filled(sp, body, body.place(("x", 1, 0)))
                        alone(sp)
                    load_x(b + 1, x_in, x_loaded)
                    sp.wait_ge(ctx_split, at(b, 2, 3))
                    alone(sp)
                    load_ctx(b + 1, 1)
                elif body.own:
                    wait_filled(sp, body, body.where[("k", 3, 1)])
                    alone(sp)
                    for i in range(3):
                        load_w(sp, i, 0, w_first[i])

            batches(sp, run)

            sp.wait_ge(pads_ready, 3)
            sp.wait_ge(table_done, 1)
            with sp.Fori(0, E) as e:
                n = sp.value_load(table[0:1, 2, ds(e, 1)], min_val=0, max_val=T)
                row = sp.snap(n + e * ROWS)
                sp.dma_start(lists[ds(row, PAD), :].rearrange("(q p) c -> p q c", p=P),
                             pad_rows[:, :, :]).then_inc(pads_stored, 16)
            sp.wait_ge(pads_stored, 16 * E)

            def store_weights():
                sp.wait_ge(fw_done, 1)
                for e in range(E):
                    sp.dma_start(weights_of[e * ROWS:e * ROWS + T, :]
                                 .rearrange("(c k) o -> c (k o)", k=GT),
                                 by_expert[e * GROUPS:(e + 1) * GROUPS, :]).then_inc(fw_stored, 16)

            def load_rows(row):
                sp.dma_start(e_rows[:, :, :],
                             lists[ds(row, CHUNK), :].rearrange("(q p) c -> p q c", p=P))\
                    .then_inc(rows_loaded, 16)

            store_weights()
            with sp.Fori(0, E) as e:
                chunks = sp.value_load(table[0:1, 0, ds(e, 1)], min_val=2, max_val=T // CHUNK)
                before = sp.value_load(table[0:1, 1, ds(e, 1)], min_val=0, max_val=MOST_CHUNKS)
                with sp.Fori(0, chunks) as j:
                    free = sp.snap(before + j + 1)
                    row = sp.snap(e * ROWS + j * CHUNK)
                    sp.wait_ge(e_turned_done, free)
                    sp.wait_ge(token_seen, free)
                    alone(sp)
                    load_rows(row)
            total = sp.value_load(table[0:1, 3, 0:1], min_val=2, max_val=MOST_CHUNKS)
            free = sp.snap(total + 1)
            all_added = sp.snap(total * (16 * ST) + 16 * ST)
            sp.wait_ge(e_turned_done, free)
            sp.wait_ge(token_seen, free)
            alone(sp)
            load_rows(0)
            sp.wait_ge(rows_loaded, 16)
            sp.wait_ge(added, all_added)
            alone(sp)

        @block.gpsimd
        def _(pool):
            def const(ins):
                ins.then_inc(consts, 1)

            const(nc.gpsimd.memset(minus_half[:, :], -0.5))
            const(nc.gpsimd.memset(ident[:, :], 1.0))
            const(nc.gpsimd.memset(same_expert[:, :], 1.0))
            const(nc.gpsimd.memset(earlier[:, :], 1.0))
            const(nc.gpsimd.memset(ones[:, :], 1.0))
            const(nc.gpsimd.memset(same_group[:, :], 0.0))
            const(nc.gpsimd.memset(rows[:, :, :], 0.0))
            const(nc.gpsimd.iota(rev[:, :], [[-1, E]], base=E, channel_multiplier=0,
                                 allow_small_or_imprecise_dtypes=True))
            const(nc.gpsimd.iota(token[:, :], [[P, QT]], base=0, channel_multiplier=1,
                                 allow_small_or_imprecise_dtypes=True))
            const(nc.gpsimd.iota(expert_row[:, :], [[ROWS, E]], base=0, channel_multiplier=0,
                                 allow_small_or_imprecise_dtypes=True))
            const(nc.gpsimd.iota(list_end[:, :], [[ROWS, E]], base=0, channel_multiplier=0,
                                 allow_small_or_imprecise_dtypes=True))
            pool.wait_ge(consts, 7)
            const(nc.gpsimd.affine_select(out=ident[:, :], in_=ident[:, :], compare_op=ALU.is_equal,
                                          fill=0.0, base=0, pattern=[[-1, P]], channel_multiplier=1))
            const(nc.gpsimd.affine_select(out=earlier[:, :], in_=earlier[:, :],
                                          compare_op=ALU.is_gt, fill=0.0, base=0, pattern=[[1, P]],
                                          channel_multiplier=-1))
            grid = same_expert[:, :].rearrange("p (e c) -> p e c", e=E)
            const(nc.gpsimd.affine_select(out=grid, in_=grid, compare_op=ALU.is_ge, fill=0.0, base=0,
                                          pattern=[[-GROUPS, E], [0, GROUPS]], channel_multiplier=1))
            pool.wait_ge(consts, 14)
            const(nc.gpsimd.affine_select(out=grid, in_=grid, compare_op=ALU.is_ge, fill=0.0,
                                          base=GROUPS - 1, pattern=[[GROUPS, E], [0, GROUPS]],
                                          channel_multiplier=-1))

            def more_consts():
                nc.gpsimd.affine_select(out=before_it[:, :], in_=same_expert[:, :],
                                        compare_op=ALU.is_gt, fill=0.0, base=0, pattern=[[1, P]],
                                        channel_multiplier=-1).then_inc(more_done, 1)
                group = same_group[:, :].rearrange("p (e c) -> p e c", e=E)
                for k in range(E):
                    pool.wait_ge(more_done, 1 + k)
                    nc.gpsimd.affine_select(out=group, in_=group, compare_op=ALU.not_equal, fill=1.0,
                                            base=-GROUPS * k, pattern=[[0, E], [-1, GROUPS]],
                                            channel_multiplier=1).then_inc(more_done, 1)

            def split_ctx(b, half):
                part = slice(half * (M // 2), (half + 1) * (M // 2))
                pool.wait_ge(ctx_loaded, at(b, 32, 16 * (half + 1)))
                alone(pool)
                nc.gpsimd.tensor_scalar(ctx_h[:, :, part], ctx_raw[:, :, :], 1.0, 1.0,
                                        ALU.mult, ALU.mult).then_inc(ctx_hi, 1)
                pool.wait_ge(ctx_hi, at(b, 2, half + 1))
                nc.gpsimd.tensor_tensor(ctx_l[:, :, part], ctx_raw[:, :, :],
                                        ctx_h[:, :, part].bitcast(F32), ALU.subtract)\
                    .then_inc(ctx_split, 1)

            def power(which, b):
                pool.wait_ge(var_done[which], at(b, 1, 1))
                nc.gpsimd.tensor_tensor(norm[:, which, 1, :], norm[:, which, 0, :], minus_half[:, :],
                                        ALU.pow).then_inc(pow_done[which], 1)

            def normalise(which, b, src, dst):
                pool.wait_ge(ln_ready[which], at(b, 1, 1))
                alone(pool)
                for q in range(QT):
                    nc.gpsimd.tensor_scalar(dst[:, q, 0:D], src[:, q, :],
                                            norm[:, which, 4, q:q + 1], norm[:, which, 5, q:q + 1],
                                            ALU.mult, ALU.add).then_inc(normed[which], 1)

            def scatter(b, i):
                q, k = i // 2, i % 2
                if i == 0:
                    pool.wait_ge(list_row_done, at(b, 1, 1))
                    alone(pool)
                nc.gpsimd.indirect_dma_start(
                    lists[:, :], bass.IndirectOffsetOnAxis(ap=list_row[:, k, q:q + 1], axis=0),
                    rows[:, q, :], None).then_inc(listed, 16)

            def run(body):
                b = body.b
                for u in range(len(body.steps)):
                    if body.own:
                        pool.wait_ge(rec_done, at(b, UNITS, u + 1))
                        alone(pool)
                        nc.gpsimd.tensor_scalar(probs[:, u % 2, :], probs[:, u % 2, :],
                                                row_rec[:, u % 2:u % 2 + 1], 1.0, ALU.mult, ALU.mult)\
                            .then_inc(scaled, 1)
                    if body.prev:
                        if u == 6:
                            power(1, b - 1)
                        if u == 7:
                            normalise(1, b - 1, x_sum, rows)
                        if UNITS - 10 <= u < UNITS - 2:
                            scatter(b - 1, u - (UNITS - 10))
                        if u == UNITS - 1:
                            pool.wait_ge(listed, at(b - 1, 16 * 2 * QT, 16 * 2 * QT))
                            alone(pool)
                    if body.own and u == 12:
                        pool.wait_ge(sum_loaded, at(b, 16, 16))
                        pool.wait_ge(bias_done, 1)
                        nc.gpsimd.tensor_tensor(
                            x_sum[:, :, :], x_sum[:, :, :],
                            bias_o[:, :].unsqueeze(1).to_broadcast([P, QT, D]), ALU.add)\
                            .then_inc(biased, 1)
                    if body.nxt:
                        if u == 16:
                            power(0, b + 1)
                        if u == 18:
                            normalise(0, b + 1, x_in, x_in)
                        if u == 20:
                            if body.own:
                                wait_filled(pool, body, body.where[("k", 3, 1)])
                            split_ctx(b + 1, 0)
                        if u == 22:
                            split_ctx(b + 1, 1)
                if body is END:
                    for i in range(2 * QT):
                        scatter(b - 1, i)

            batches(pool, run)

            def split_w(e, i, parity):
                if isinstance(e, int) and e == 0:
                    pool.wait_ge(w_first[i], 16)
                else:
                    pool.wait_ge(w_loaded[i], at(e, 16, 0))
                    alone(pool)
                nc.gpsimd.tensor_scalar(w_h[parity][i][:, :], w_raw[i][:, :], 1.0, 1.0,
                                        ALU.mult, ALU.mult).then_inc(w_hi, 1)
                pool.wait_ge(w_hi, at(e, 3, i + 1))
                nc.gpsimd.tensor_tensor(w_l[parity][i][:, :], w_raw[i][:, :],
                                        w_h[parity][i][:, :].bitcast(F32), ALU.subtract)\
                    .then_inc(w_split, 1)

            def reload_w(e, i):
                pool.wait_ge(w_split, at(e - 1, 3, i + 1))
                alone(pool)
                load_w(pool, i, e, w_loaded[i])

            more_consts()
            pool.wait_ge(listed, 16 * 2 * QT * B)
            pool.wait_ge(sum_stored, 16 * B)
            nc.gpsimd.memset(zeros[:, :, :], 0.0).then_inc(pads_ready, 1)
            nc.gpsimd.memset(pad_rows[:, :, :], 0.0).then_inc(pads_ready, 1)
            pool.wait_ge(pads_ready, 2)
            nc.gpsimd.iota(pad_rows[:, :, D:D + 1], [[P, PAD // P], [0, 1]], base=T,
                           channel_multiplier=1, allow_small_or_imprecise_dtypes=True)\
                .then_inc(pads_ready, 1)
            nc.gpsimd.dma_start(out[T:ROWS, :].rearrange("(q p) d -> p q d", p=P), zeros[:, :, :])\
                .then_inc(added, 16)
            nc.gpsimd.dma_start(weights_of.rearrange("(e t) o -> e (t o)", e=E)[:, T:ROWS],
                                zeros[0:E, 0:PAD // D, :].rearrange("p q d -> p (q d)"))\
                .then_inc(added, 16)
            for i in range(3):
                split_w(0, i, 0)
                reload_w(1, i)
            pool.wait_ge(added, 16 * ST)
            pool.wait_ge(fw_stored, 16 * E)
            pool.wait_ge(pads_stored, 16 * E)

            def gather(g):
                pool.wait_ge(token_done, g + 1)
                alone(pool)
                for st in range(ST):
                    nc.gpsimd.indirect_dma_start(
                        y_weight[:, st:st + 1], None, weights_of[:, :],
                        bass.IndirectOffsetOnAxis(ap=y_at[:, st:st + 1], axis=0))\
                        .then_inc(weight_here, 16)

            def scatter_add(g):
                pool.wait_ge(added, g * (16 * ST) + 16 * ST)
                for st in range(ST):
                    pool.wait_ge(y_done[st], g + 2)
                    alone(pool)
                    nc.gpsimd.indirect_dma_start(
                        out[:, :], bass.IndirectOffsetOnAxis(ap=y_token[:, st:st + 1], axis=0),
                        y[:, st, :], None, compute_op=ALU.add).then_inc(added, 16)

            def expert(e, parity, has_next, has_second):
                chunks = pool.value_load(table[0:1, 0, ds(e, 1)], min_val=2, max_val=T // CHUNK)
                before = pool.value_load(table[0:1, 1, ds(e, 1)], min_val=0,
                                         max_val=MOST_CHUNKS)
                first = pool.snap(before + 0)
                if has_next:
                    split_w(e + 1, 0, 1 - parity)
                gather(first)
                if has_next:
                    split_w(e + 1, 1, 1 - parity)
                scatter_add(first)
                if has_next:
                    split_w(e + 1, 2, 1 - parity)
                if has_second:
                    for i in range(3):
                        reload_w(e + 2, i)
                with pool.Fori(1, chunks) as j:
                    g = pool.snap(before + j)
                    gather(g)
                    scatter_add(g)

            pool.wait_ge(table_done, 1)
            with pool.Fori(0, E // 2 - 1) as pair:
                for parity in range(2):
                    expert(2 * pair + parity, parity, True, True)
            for parity in range(2):
                expert(E - 2 + parity, parity, parity == 0, False)

        def passes(out_, st, mv, start, stop):
            (sh, sl), (mh, ml) = st, mv
            nc.tensor.matmul(out_, sh, mh, start=start, stop=False)
            nc.tensor.matmul(out_, sh, ml, start=False, stop=False)
            return nc.tensor.matmul(out_, sl, mh, start=False, stop=stop)

        @block.tensor
        def _(pe):
            pe.sem_inc(e_turned_done, 1)
            pe.sem_inc(ffn1_done, 1)
            pe.sem_inc(ffn2_done, 1)

            def make_scores(body, u):
                b, h, q = body.b, u // QT, u % QT
                buf, ab = (h // 2) % 2, h % 2
                if u % (2 * QT) == 0:
                    wait_all_drained(pe, body, [body.place(("q", h // 2, 0))] +
                                     [body.place(("k", h // 2, keys)) for keys in range(2)])
                until(pe, exp_done, at(b, UNITS, u - 1))
                for part in (q_h, q_l):
                    for half in range(2):
                        cols = slice(half * 512, (half + 1) * 512)
                        last = nc.tensor.matmul(scores[:, u % 2, cols],
                                                part[:, buf, ab, q * P:(q + 1) * P],
                                                k_st[:, buf, ab, cols],
                                                start=part is q_h, stop=part is q_l)
                last.then_inc(scores_done, 1)

            def turn(body, n):
                pe.wait_ge(scaled, at(body.b, UNITS, n + 1))
                for j in range(2):
                    until(pe, pt_lo, at(body.b, 2 * UNITS, 2 * n - 1 + j))
                    for i in range(4):
                        kt = 4 * j + i
                        last = nc.tensor.transpose(turned[:, j, i * P:(i + 1) * P],
                                                   probs[:, n % 2, kt * P:(kt + 1) * P], ident[:, :])
                    last.then_inc(turned_done, 1)

            def wait_for_job(body, u, what):
                kind, i, j = what
                b = body.b
                reads = []
                if kind == "o":
                    m = i - 2 * H if u < 4 else i
                    pe.wait_ge(pt_lo, at(b, 2 * UNITS, 4 * m + 4))
                    if i % H == 0:
                        reads = [body.place(("v", i // H, keys)) for keys in range(4)]
                if kind == "w":
                    if body is FIRST and i == 0 and j == 0:
                        pe.wait_ge(weights_split, 5)
                    reads = [body.where[("o", H * i + H - 2 + j, 0)]]
                if kind == "x":
                    pe.wait_ge(normed[0], at(b + 1, QT, QT))
                if kind == "v" and i == 0 and j % 2 == 0:
                    pe.wait_ge(ctx_split, at(b + 1, 2, 1 + j // 2))
                    if body is START:
                        pe.wait_ge(weights_split, 3)
                if kind == "q" and i == 0:
                    reads = [body.where[("x", 0, 0)], body.where[("x", 1, 0)]]
                if kind == "h":
                    pe.wait_ge(normed[1], at(b - 1, QT, 2 * i + 2))
                if kind == "l":
                    reads = [body.where[("h", 0, 0)], body.where[("h", 1, 0)]]
                if kind == "r":
                    pe.wait_ge(chosen_done, at(b - 1, 1, 1))
                return reads

            def do_job(what, bank):
                kind, i, j = what
                if kind == "q":
                    cols = slice(i * P, (i + 1) * P)
                    for kc in range(KC):
                        last = passes(bank, (wq_h[:, kc, cols], wq_l[:, kc, cols]),
                                      (xt_h[:, kc, :], xt_l[:, kc, :]), kc == 0, kc == KC - 1)
                if kind == "k":
                    cols, keys = slice(i * P, (i + 1) * P), slice(j * 512, (j + 1) * 512)
                    for kc in range(KC):
                        last = passes(bank, (wk_h[:, kc, cols], wk_l[:, kc, cols]),
                                      (ctx_h[:, kc, keys], ctx_l[:, kc, keys]), kc == 0, kc == KC - 1)
                if kind == "v":
                    cols = slice(i * 256, (i + 1) * 256)
                    for t in range(2):
                        keys = slice((2 * j + t) * P, (2 * j + t + 1) * P)
                        for kc in range(KC):
                            last = passes(bank[:, t * 256:(t + 1) * 256],
                                          (ctx_h[:, kc, keys], ctx_l[:, kc, keys]),
                                          (wv_h[:, kc, cols], wv_l[:, kc, cols]), kc == 0, kc == KC - 1)
                if kind == "w":
                    for t in range(2):
                        toks = slice((2 * j + t) * P, (2 * j + t + 1) * P)
                        for h in range(H // 2):
                            head = i * (H // 2) + h
                            last = passes(bank[:, t * D:(t + 1) * D],
                                          (ot_h[:, h, toks], ot_l[:, h, toks]),
                                          (wo_h[:, head, :], wo_l[:, head, :]),
                                          h == 0, h == H // 2 - 1)
                if kind == "x":
                    for q in range(QT):
                        last = nc.tensor.transpose(bank[:, q * P:(q + 1) * P],
                                                   x_in[:, q, i * P:(i + 1) * P], ident[:, :])
                if kind == "h":
                    for t in range(2):
                        for kc in range(KC):
                            last = nc.tensor.transpose(
                                bank[:, (t * KC + kc) * P:(t * KC + kc + 1) * P],
                                rows[:, 2 * i + t, kc * P:(kc + 1) * P], ident[:, :])
                if kind == "l":
                    for q in range(QT):
                        for kc in range(KC):
                            last = nc.tensor.matmul(bank[:, q * E:(q + 1) * E], h_t[:, q, kc, :],
                                                    rw[:, kc, :], start=kc == 0, stop=kc == KC - 1)
                if kind == "r":
                    for q in range(QT):
                        nc.tensor.matmul(bank[:, q * E:(q + 1) * E], earlier[:, :], chosen[:, q, :],
                                         start=True, stop=q == 0)
                        for before in range(q):
                            nc.tensor.matmul(bank[:, q * E:(q + 1) * E], ones[:, :],
                                             chosen[:, before, :], start=False, stop=before == q - 1)
                    for q in range(QT):
                        last = nc.tensor.matmul(bank[:, QT * E:(QT + 1) * E], ones[:, :],
                                                chosen[:, q, :], start=q == 0, stop=q == QT - 1)
                if kind == "o":
                    h, m = i // 2, i % 2
                    for kt in range(KT):
                        for part in (pt_h, pt_l):
                            last = nc.tensor.matmul(bank[:, 0:2 * P], v_hl[:, kt, h, :],
                                                    part[:, m, kt, :],
                                                    start=kt == 0 and part is pt_h,
                                                    stop=kt == KT - 1 and part is pt_l)
                last.then_inc(filled, 1)

            def run(body):
                for u, jobs in enumerate(body.steps):
                    if body.own:
                        make_scores(body, u)
                    if body.prev if u < 2 else body.own:
                        turn(body, u - 2)
                    for what, c in jobs:
                        reads = wait_for_job(body, u, what)
                        wait_all_drained(pe, body, reads + [c - 2])
                        do_job(what, ring[:, c % 2, :])

            pe.wait_ge(consts, CONSTS)
            pe.wait_ge(small_loaded, 64)
            batches(pe, run)

            pe.wait_ge(list_row_done, B)
            for half in range(2):
                last = nc.tensor.transpose(misc[:, half * P:(half + 1) * P],
                                           assigned[:, :, half::2], ident[:, :])
            last.then_inc(gathered, 1)
            pe.wait_ge(more_done, E + 1)
            with pe.Fori(0, WEIGHT_BITS) as i:
                pe.wait_ge(counted, i + 1)
                nc.tensor.matmul(misc[:, 0:1], same_expert[:, :], counts[:, 0:1],
                                 start=True, stop=True).then_inc(summed, 1)
            pe.wait_ge(counted, WEIGHT_BITS + 1)
            nc.tensor.matmul(misc[:, 0:1], same_expert[:, :], counts[:, 1:2], start=True, stop=True)
            nc.tensor.matmul(misc[:, 1:2], before_it[:, :], counts[:, 2:3], start=True, stop=True)\
                .then_inc(summed, 1)
            pe.wait_ge(kept, 1)
            nc.tensor.matmul(misc[:, GT:2 * GT], same_group[:, :], work[:, 3, :],
                             start=True, stop=True).then_inc(wsum_done, 1)

            def turn_rows(loaded):
                pe.wait_ge(rows_loaded, loaded)
                for kc in range(KC):
                    for st in range(ST):
                        last = nc.tensor.transpose(e_turned[:, kc, st * P:(st + 1) * P],
                                                   e_rows[:, st, kc * P:(kc + 1) * P], ident[:, :])
                last.then_inc(e_turned_done, 1)

            def up(g, c, parity):
                pe.wait_ge(act_done, g * FC + c + 1)
                for i in range(2):
                    for kc in range(KC):
                        cols = slice(kc * FF + c * P, kc * FF + (c + 1) * P)
                        last = passes(ffn1[:, c % 4, i, :],
                                      (w_h[parity][i][:, cols], w_l[parity][i][:, cols]),
                                      (et_h[:, kc, :], et_l[:, kc, :]), kc == 0, kc == KC - 1)
                last.then_inc(ffn1_done, 1)

            def down(g, c, parity):
                pe.wait_ge(act_lo, g * FC + c + 1)
                for st in range(ST):
                    if c == 0:
                        pe.wait_ge(y_done[st], g + 1)
                    toks, cols = slice(st * P, (st + 1) * P), slice(c * D, (c + 1) * D)
                    last = passes(ffn2[:, st, 0:D], (act_h[:, c, toks], act_l[:, c, toks]),
                                  (w_h[parity][2][:, cols], w_l[parity][2][:, cols]),
                                  c == 0, c == FC - 1)
                    if c == FC - 1:
                        last.then_inc(ffn2_done, 1)

            def chunk(g, parity, follows):
                pe.wait_ge(et_lo, g + 1)
                for c in range(FC):
                    up(g, c, parity)
                    if c == 0 and follows:
                        down(g - 1, FC - 1, parity)
                    if c == FC - 2:
                        turn_rows(g * 16 + 32)
                    if c >= 2:
                        down(g, c - 2, parity)
                down(g, FC - 2, parity)

            turn_rows(16)
            pe.wait_ge(table_done, 1)
            with pe.Fori(0, E // 2) as pair:
                for parity in range(2):
                    e = 2 * pair + parity
                    chunks = pe.value_load(table[0:1, 0, ds(e, 1)], min_val=2, max_val=T // CHUNK)
                    before = pe.value_load(table[0:1, 1, ds(e, 1)], min_val=0, max_val=MOST_CHUNKS)
                    pe.wait_ge(w_split, at(e, 3, 3))
                    chunk(pe.snap(before + 0), parity, False)
                    with pe.Fori(1, chunks) as j:
                        chunk(pe.snap(before + j), parity, True)
                    down(pe.snap(before + chunks - 1), FC - 1, parity)

        @block.scalar
        def _(act):
            act.sem_inc(y_done[0], 1)

            def hi(dst, src):
                return nc.scalar.activation(dst, src, ACT.Copy)

            def split_raw(i, raw, dst, loads):
                act.wait_ge(raw_loaded[i], 16 * loads)
                hi(dst, raw).then_inc(raw_hi, 1)

            def drain(body, u, what, c):
                kind, i, j = what
                if kind in "lrw":
                    return
                bank = ring[:, c % 2, :]
                wait_filled(act, body, c)
                if kind == "h":
                    hi(x_in[:, 2 * i:2 * i + 2, :].rearrange("p q d -> p (q d)"), bank)\
                        .then_inc(drained[c % 2], 1)
                    return
                if kind == "q":
                    for ab in range(2):
                        for half in range(2):
                            last = hi(q_h[half * DH:(half + 1) * DH, i % 2, ab, :],
                                      bank[ab * DH:(ab + 1) * DH, :])
                if kind == "k":
                    for ab in range(2):
                        head = slice(ab * DH, (ab + 1) * DH)
                        last = hi(k_st[head, i % 2, ab, j * 512:(j + 1) * 512], bank[head, :])
                if kind == "v":
                    last = hi(v_hl[:, 2 * j:2 * j + 2, 4 * i:4 * i + 4, 0:DH],
                              bank.rearrange("p (t h d) -> p t h d", t=2, d=DH))
                if kind == "o":
                    toks = slice((i % 2) * 2 * P, (i % 2 + 1) * 2 * P)
                    last = hi(ot_h[:, (i // 2) % 4, toks], bank[:, 0:2 * P])
                if kind == "x":
                    last = hi(xt_h[:, i, :], bank)
                last.then_inc(hi_done[kind], 1)

            def run(body):
                b = body.b
                for u, jobs in enumerate(body.steps):
                    if body is START and u == 19:
                        flat = x_sum[:, :, :].rearrange("p q d -> p (q d)")
                        for i, (dst, raw) in enumerate(((wq_h, probs[:, 0, :]), (wk_h, probs[:, 1, :]),
                                                        (wv_h, flat))):
                            split_raw(i, raw, dst[:, :, :].rearrange("p c n -> p (c n)"), 1)
                    if body is FIRST and u in (5, 8):
                        half = (u - 5) // 3
                        split_raw(3 + half, x_sum[:, :, :], wo_h[:, half * 4:half * 4 + 4, :], 2)
                    if body.prev if u < 2 else body.own:
                        n = u - 2
                        toks = slice((n % 2) * P, (n % 2 + 1) * P)
                        for j in range(2):
                            act.wait_ge(turned_done, at(b, 2 * UNITS, 2 * n + j + 1))
                            hi(pt_h[:, (n // 2) % 2, 4 * j:4 * j + 4, toks],
                               turned[:, j, :].rearrange("p (k t) -> p k t", t=P)).then_inc(pt_hi, 1)
                    if body.own:
                        act.wait_ge(neg_done, at(b, UNITS, u + 1))
                        nc.scalar.activation(probs[:, u % 2, :], scores[:, u % 2, :], ACT.Exp,
                                             bias=neg_max[:, u % 2:u % 2 + 1], scale=SCALE,
                                             accum_out=row_sum[:, u % 2:u % 2 + 1])\
                            .then_inc(exp_done, 1)
                    if body.prev and u == 14:
                        wait_drained(act, body, body.where[("l", 0, 0)])
                        nc.scalar.activation(gate[:, 1, :, :], gate[:, 0, :, :], ACT.Exp)\
                            .then_inc(gate_exp, 1)
                    for what, c in jobs:
                        drain(body, u, what, c)

            act.wait_ge(small_loaded, 64)
            nc.scalar.activation(tanh_g[:, :], tanh_g[:, :], ACT.Tanh).then_inc(tanh_done, 1)
            batches(act, run)

            def finish(n):
                act.wait_ge(weight_here, n * (16 * ST))
                act.wait_ge(ffn2_done, n * ST)
                act.wait_ge(added, n * (16 * ST))
                nc.scalar.activation(y[:, 0, :], ffn2[:, 0, 0:D], ACT.Copy,
                                     scale=y_weight[:, 0:1]).then_inc(y_done[0], 1)

            def chunk(g, follows):
                act.wait_ge(e_turned_done, g + 2)
                act.wait_ge(ffn1_done, g * FC + 1)
                hi(et_h[:, :, :], e_turned[:, :, :]).then_inc(et_hi, 1)
                for c in range(FC):
                    act.wait_ge(ffn1_done, g * FC + c + 2)
                    nc.scalar.activation(silu[:, :], ffn1[:, c % 4, 1, :], ACT.Silu)\
                        .then_inc(silu_done, 1)
                    act.wait_ge(act_done, g * FC + c + 5)
                    hi(act_h[:, c, :], act_f[:, c % 2, :]).then_inc(act_hi, 1)
                    if c == 0 and follows:
                        finish(g)

            act.wait_ge(table_done, 1)
            with act.Fori(0, E) as e:
                chunks = act.value_load(table[0:1, 0, ds(e, 1)], min_val=2, max_val=T // CHUNK)
                before = act.value_load(table[0:1, 1, ds(e, 1)], min_val=0, max_val=MOST_CHUNKS)
                chunk(act.snap(before + 0), False)
                with act.Fori(1, chunks) as j:
                    chunk(act.snap(before + j), True)
                finish(act.snap(before + chunks))

        @block.vector
        def _(v):
            v.sem_inc(y_done[1], 1)
            v.sem_inc(token_seen, 1)
            v.sem_inc(act_done, 4)

            def lo(dst, src, hi_part):
                return nc.vector.tensor_tensor(dst, src, hi_part.bitcast(F32), ALU.subtract)

            def split_raw(i, raw, dst, hi_part):
                v.wait_ge(raw_hi, i + 1)
                lo(dst, raw, hi_part).then_inc(weights_split, 1)

            def layer_stats(which, b, src):
                for q in range(QT):
                    last = nc.vector.bn_stats(stats[:, which, q, :], src[:, q, :])
                last.then_inc(ln_seq[which], 1)
                v.wait_ge(ln_seq[which], at(b, 4, 1))
                alone(v)
                for q in range(QT):
                    last = nc.vector.bn_aggr(mean_var[:, which, q, :], stats[:, which, q, :])
                last.then_inc(ln_seq[which], 1)
                v.wait_ge(ln_seq[which], at(b, 4, 2))
                nc.vector.tensor_scalar(norm[:, which, 0, :], mean_var[:, which, :, 1], LN_EPS, None,
                                        ALU.add).then_inc(var_done[which], 1)

            def layer_scale(which, b):
                var, y0, w0, w1, scale, shift = (norm[:, which, k, :] for k in range(6))
                v.wait_ge(pow_done[which], at(b, 1, 1))
                nc.vector.scalar_tensor_tensor(w0, y0, -0.5, y0, ALU.mult, ALU.mult)\
                    .then_inc(ln_seq[which], 1)
                v.wait_ge(ln_seq[which], at(b, 4, 3))
                nc.vector.tensor_tensor(w1, w0, var, ALU.mult).then_inc(ln_seq[which], 1)
                v.wait_ge(ln_seq[which], at(b, 4, 4))
                nc.vector.scalar_tensor_tensor(scale, w1, 1.5, y0, ALU.add, ALU.mult)\
                    .then_inc(scaled_ln[which], 1)
                v.wait_ge(scaled_ln[which], at(b, 1, 1))
                nc.vector.scalar_tensor_tensor(shift, mean_var[:, which, :, 0], -1.0, scale,
                                               ALU.mult, ALU.mult).then_inc(ln_ready[which], 1)

            def route(b):
                def after(n):
                    v.wait_ge(gate_seq, at(b, GATE_STEPS, n))

                def step(ins):
                    ins.then_inc(gate_seq, 1)

                def wide(t):
                    return t.unsqueeze(2).to_broadcast([P, QT, E])

                ranks = rev[:, :].unsqueeze(1).to_broadcast([P, QT, E])
                expd, prob, equal, others, mask, part = (gate[:, k, :, :] for k in range(1, 7))
                best = gate1[:, 0:2, :]
                v.wait_ge(gate_exp, at(b, 1, 1))
                step(nc.vector.reduce_sum(gate1[:, 3, :], expd, AX.X))
                after(2)
                step(nc.vector.reciprocal(gate1[:, 4, :], gate1[:, 3, :]))
                after(3)
                step(nc.vector.tensor_tensor(prob, expd, wide(gate1[:, 4, :]), ALU.mult))
                after(4)
                for k, of in enumerate((prob, others)):
                    step(nc.vector.reduce_max(gate1[:, k, :], of, AX.X))
                    after(5 + 6 * k)
                    step(nc.vector.tensor_tensor(equal, of, wide(gate1[:, k, :]), ALU.is_equal))
                    after(6 + 6 * k)
                    step(nc.vector.tensor_tensor(part, equal, ranks, ALU.mult))
                    after(7 + 6 * k)
                    step(nc.vector.reduce_max(gate1[:, 5, :], part, AX.X))
                    after(8 + 6 * k)
                    step(nc.vector.tensor_tensor(oh[:, k, :, :], ranks, wide(gate1[:, 5, :]),
                                                 ALU.is_equal))
                    after(9 + 6 * k)
                    if k == 0:
                        step(nc.vector.scalar_tensor_tensor(others, oh[:, 0, :, :], -2.0, prob,
                                                            ALU.mult, ALU.add))
                        after(10)
                nc.vector.tensor_tensor(chosen[:, :, :], oh[:, 0, :, :], oh[:, 1, :, :], ALU.add)\
                    .then_inc(chosen_done, 1)
                step(nc.vector.scalar_tensor_tensor(mask, oh[:, 0, :, :], -1.0, oh[:, 1, :, :],
                                                    ALU.add, ALU.add))
                step(nc.vector.tensor_tensor(gate1[:, 6, :], gate1[:, 0, :], gate1[:, 1, :], ALU.add))
                after(17)
                step(nc.vector.tensor_scalar(gate1[:, 7, :], gate1[:, 6, :], EPS, None, ALU.max))
                after(18)
                step(nc.vector.reciprocal(gate1[:, 3, :], gate1[:, 7, :]))
                after(19)
                step(nc.vector.tensor_tensor(
                    gate1[:, 4:6, :], best, gate1[:, 3, :].unsqueeze(1).to_broadcast([P, 2, QT]),
                    ALU.mult))
                after(20)
                step(nc.vector.tensor_tensor(
                    oh_x[:, :, :, :], oh[:, :, :, :],
                    gate1[:, 4:6, :].unsqueeze(3).to_broadcast([P, 2, QT, E]), ALU.mult))
                after(21)
                step(nc.vector.tensor_tensor(part, mask, oh_x[:, 0, :, :], ALU.add))
                after(22)
                step(nc.vector.tensor_tensor(
                    assigned[:, :, ds(b * QT, QT)].rearrange("p e q -> p q e"), part,
                    oh_x[:, 1, :, :], ALU.add))

            def place_rows(body, c):
                b = body.b - 1

                def after(n):
                    v.wait_ge(rank_seq, at(b, RANK_STEPS, n))

                bank = ring[:, c % 2, :]
                wait_filled(v, body, c)
                nc.vector.tensor_tensor(gate[:, 7, :, :],
                                        bank[:, 0:QT * E].rearrange("p (q e) -> p q e", e=E),
                                        list_end[:, :].unsqueeze(1).to_broadcast([P, QT, E]),
                                        ALU.add).then_inc(rank_seq, 1)
                nc.vector.tensor_copy(rows[:, :, D], token[:, :]).then_inc(rank_seq, 1)
                after(2)
                nc.vector.tensor_tensor(list_end[:, :], list_end[:, :],
                                        bank[:, QT * E:(QT + 1) * E], ALU.add)\
                    .then_inc(drained[c % 2], 1)
                nc.vector.tensor_scalar(token[:, :], token[:, :], float(N), None, ALU.add)\
                    .then_inc(rank_seq, 1)
                nc.vector.tensor_tensor(oh_x[:, :, :, :], oh[:, :, :, :],
                                        gate[:, 7, :, :].unsqueeze(1).to_broadcast([P, 2, QT, E]),
                                        ALU.mult).then_inc(rank_seq, 1)
                after(4)
                nc.vector.reduce_sum(row_f[:, :, :], oh_x[:, :, :, :], AX.X).then_inc(rank_seq, 1)
                after(5)
                nc.vector.tensor_copy(list_row[:, :, :], row_f[:, :, :]).then_inc(list_row_done, 1)

            def drain(body, u, what, c):
                kind, i, j = what
                bank = ring[:, c % 2, :]
                if kind == "h":
                    return
                if kind == "r":
                    place_rows(body, c)
                    return
                if kind == "l":
                    logits = bank[:, 0:QT * E].rearrange("p (q e) -> p q e", e=E)
                    wait_filled(v, body, c)
                    nc.vector.reduce_max(gate1[:, 2, :], logits, AX.X).then_inc(gate_seq, 1)
                    v.wait_ge(gate_seq, at(body.b - 1, GATE_STEPS, 1))
                    nc.vector.tensor_tensor(gate[:, 0, :, :], logits,
                                            gate1[:, 2, :].unsqueeze(2).to_broadcast([P, QT, E]),
                                            ALU.subtract).then_inc(drained[c % 2], 1)
                    return
                if kind == "w":
                    if i == 0 and j == 0:
                        v.wait_ge(biased, at(body.b, 1, 1))
                        v.wait_ge(tanh_done, 1)
                    if i == 1:
                        wait_drained(v, body, body.before.where[("w", 0, j)] - RING)
                    wait_filled(v, body, c)
                    part = x_sum[:, 2 * j:2 * j + 2, :].rearrange("p q d -> p (q d)")
                    nc.vector.scalar_tensor_tensor(part, bank, tanh_g[:, 0:1], part,
                                                   ALU.mult, ALU.add).then_inc(drained[c % 2], 1)
                    return
                b, n = of_batch(body, what, u)
                wait_hi(v, kind, b, n)
                if kind == "q":
                    for ab in range(2):
                        for half in range(2):
                            head = slice(ab * DH, (ab + 1) * DH)
                            last = lo(q_l[half * DH:(half + 1) * DH, i % 2, ab, :], bank[head, :],
                                      q_h[head, i % 2, ab, :])
                if kind == "k":
                    for ab in range(2):
                        head, other = slice(ab * DH, (ab + 1) * DH), slice((1 - ab) * DH, (2 - ab) * DH)
                        keys = slice(j * 512, (j + 1) * 512)
                        last = lo(k_st[other, i % 2, ab, keys], bank[head, :],
                                  k_st[head, i % 2, ab, keys])
                if kind == "v":
                    part = v_hl[:, 2 * j:2 * j + 2, 4 * i:4 * i + 4, :]
                    last = lo(part[:, :, :, DH:P], bank.rearrange("p (t h d) -> p t h d", t=2, d=DH),
                              part[:, :, :, 0:DH])
                if kind == "o":
                    toks = slice((i % 2) * 2 * P, (i % 2 + 1) * 2 * P)
                    last = lo(ot_l[:, (i // 2) % 4, toks], bank[:, 0:2 * P],
                              ot_h[:, (i // 2) % 4, toks])
                if kind == "x":
                    last = lo(xt_l[:, i, :], bank, xt_h[:, i, :])
                last.then_inc(drained[c % 2], 1)

            def run(body):
                b = body.b
                for u, jobs in enumerate(body.steps):
                    k = u % 2
                    if body is START and u == 19:
                        flat = x_sum[:, :, :].rearrange("p q d -> p (q d)")
                        for i, (dst, hp, raw) in enumerate(((wq_l, wq_h, probs[:, 0, :]),
                                                            (wk_l, wk_h, probs[:, 1, :]),
                                                            (wv_l, wv_h, flat))):
                            split_raw(i, raw, dst[:, :, :].rearrange("p c n -> p (c n)"),
                                      hp[:, :, :].rearrange("p c n -> p (c n)"))
                        v.wait_ge(tanh_done, 1)
                        nc.vector.tensor_scalar(bias_o[:, :], bias_o[:, :], tanh_g[:, 0:1], None,
                                                ALU.mult).then_inc(bias_done, 1)
                    if body is FIRST and u in (5, 8):
                        half = (u - 5) // 3
                        part = slice(half * 4, half * 4 + 4)
                        split_raw(3 + half, x_sum[:, :, :], wo_l[:, part, :], wo_h[:, part, :])
                    if body.own:
                        v.wait_ge(scores_done, at(b, UNITS, u + 1))
                        nc.vector.reduce_max(row_max[:, k:k + 1],
                                             scores[:, k, :].rearrange("p (a c) -> p a c", a=2),
                                             AX.XY).then_inc(max_done, 1)
                        v.wait_ge(max_done, at(b, UNITS, u + 1))
                        nc.vector.tensor_scalar(neg_max[:, k:k + 1], row_max[:, k:k + 1], -SCALE, None,
                                                ALU.mult).then_inc(neg_done, 1)
                    if body.prev if u < 2 else body.own:
                        n = u - 2
                        toks = slice((n % 2) * P, (n % 2 + 1) * P)
                        for j in range(2):
                            v.wait_ge(pt_hi, at(b, 2 * UNITS, 2 * n + j + 1))
                            lo(pt_l[:, (n // 2) % 2, 4 * j:4 * j + 4, toks],
                               turned[:, j, :].rearrange("p (k t) -> p k t", t=P),
                               pt_h[:, (n // 2) % 2, 4 * j:4 * j + 4, toks]).then_inc(pt_lo, 1)
                    if body.own:
                        v.wait_ge(exp_done, at(b, UNITS, u + 1))
                        nc.vector.reciprocal(row_rec[:, k:k + 1], row_sum[:, k:k + 1])\
                            .then_inc(rec_done, 1)
                    for what, c in jobs:
                        drain(body, u, what, c)
                    if body.prev:
                        if u == 6:
                            wait_drained(v, body, body.where[("w", 1, 1)])
                            layer_stats(1, b - 1, x_sum)
                        if u == 7:
                            layer_scale(1, b - 1)
                        if u == 14:
                            route(b - 1)
                    if body.nxt:
                        if u == 15:
                            v.wait_ge(x_loaded, at(b + 1, 16, 16))
                            layer_stats(0, b + 1, x_in)
                        if u == 17:
                            layer_scale(0, b + 1)

            v.wait_ge(consts, CONSTS)
            batches(v, run)

            def own(ins):
                ins.then_inc(search_seq, 1)

            v.wait_ge(drained[END.where[("r", 0, 0)] % 2],
                      at(B, RING // 2, END.where[("r", 0, 0)] // 2 + 1))
            own(nc.vector.tensor_tensor(table_f[:, 0, :], list_end[:, :], expert_row[:, :],
                                        ALU.subtract))
            v.wait_ge(search_seq, 1)
            own(nc.vector.tensor_copy(table[:, 2, :], table_f[:, 0, :]))
            own(nc.vector.tensor_scalar(table[:, 1, :], table_f[:, 0, :], float(CHUNK - 1), None,
                                        ALU.add))
            v.wait_ge(search_seq, 3)
            own(nc.vector.tensor_scalar(table[:, 3, :], table[:, 1, :], CHUNK.bit_length() - 1, None,
                                        ALU.arith_shift_right))
            v.wait_ge(search_seq, 4)
            own(nc.vector.tensor_scalar(table[:, 0, :], table[:, 3, :], 2.0, None, ALU.max))
            own(nc.vector.tensor_scalar(table_f[:, 0, :], table[:, 3, :], 2.0, None, ALU.max))
            v.wait_ge(search_seq, 6)
            own(nc.vector.tensor_tensor_scan(table_f[:, 1, :], table_f[:, 0, :], table_f[:, 0, :], 0.0,
                                             ALU.add, ALU.bypass))
            v.wait_ge(search_seq, 7)
            own(nc.vector.tensor_tensor(table[:, 1, :], table_f[:, 1, :], table_f[:, 0, :],
                                        ALU.subtract))
            nc.vector.tensor_copy(table[:, 3, 0:1], table_f[:, 1, E - 1:E]).then_inc(table_done, 1)

            own(nc.vector.memset(threshold[:, :], 0))
            own(nc.vector.memset(bit_f[:, :], float(1 << (WEIGHT_BITS - 1))))
            v.wait_ge(search_seq, 10)
            own(nc.vector.tensor_copy(bit[:, :], bit_f[:, :]))
            v.wait_ge(gathered, 1)
            own(nc.vector.tensor_copy(by_expert[:, :], misc[:, 0:GT]))
            v.wait_ge(search_seq, 12)
            with v.Fori(0, WEIGHT_BITS) as i:
                def after(n):
                    v.wait_ge(search_bits, i * 5 + n)

                def step(ins):
                    ins.then_inc(search_bits, 1)

                v.wait_ge(search_seq, 12)
                step(nc.vector.tensor_tensor(candidate[:, :], threshold[:, :], bit[:, :],
                                             ALU.bitwise_or))
                after(1)
                nc.vector.tensor_scalar(work[:, 0, :], by_expert[:, :], candidate[:, :].bitcast(F32),
                                        0.0, ALU.is_ge, ALU.add, accum_out=counts[:, 0:1])\
                    .then_inc(counted, 1)
                v.wait_ge(summed, i + 1)
                step(nc.vector.tensor_scalar(raised[:, :], misc[:, 0:1], float(CAPACITY),
                                             bit_f[:, 0:1], ALU.is_ge, ALU.mult))
                after(2)
                step(nc.vector.tensor_tensor(threshold[:, :], threshold[:, :], raised[:, :],
                                             ALU.bitwise_or))
                step(nc.vector.tensor_scalar(bit[:, :], bit[:, :], 1, None, ALU.logical_shift_right))
                step(nc.vector.tensor_scalar(bit_f[:, :], bit_f[:, :], 0.5, None, ALU.mult))
                after(5)

            above, equal, rank, keep, room = (work[:, k, :] for k in range(5))
            lowest = threshold[:, :].bitcast(F32)
            nc.vector.tensor_scalar(above, by_expert[:, :], lowest, 0.0, ALU.is_gt, ALU.add,
                                    accum_out=counts[:, 1:2])
            nc.vector.tensor_scalar(equal, by_expert[:, :], lowest, 0.0, ALU.is_equal, ALU.add,
                                    accum_out=counts[:, 2:3]).then_inc(counted, 1)
            v.wait_ge(counted, WEIGHT_BITS + 1)
            own(nc.vector.tensor_tensor_scan(rank, equal, equal, 0.0, ALU.add, ALU.bypass))
            v.wait_ge(summed, WEIGHT_BITS + 1)
            own(nc.vector.tensor_copy(counts[:, 3:4], misc[:, 0:1]))
            v.wait_ge(search_seq, 14)
            own(nc.vector.tensor_tensor(counts[:, 0:1], misc[:, 1:2], counts[:, 3:4], ALU.add))
            v.wait_ge(search_seq, 15)
            own(nc.vector.tensor_scalar(room, rank, counts[:, 0:1], float(CAPACITY),
                                        ALU.add, ALU.is_le))
            v.wait_ge(search_seq, 16)
            own(nc.vector.tensor_tensor(rank, equal, room, ALU.mult))
            v.wait_ge(search_seq, 17)
            own(nc.vector.tensor_tensor(room, rank, above, ALU.add))
            v.wait_ge(search_seq, 18)
            nc.vector.tensor_tensor(keep, by_expert[:, :], room, ALU.mult).then_inc(kept, 1)
            v.wait_ge(wsum_done, 1)
            own(nc.vector.tensor_scalar(rank, misc[:, GT:2 * GT], EPS, None, ALU.max))
            v.wait_ge(search_seq, 19)
            own(nc.vector.reciprocal(room, rank))
            v.wait_ge(search_seq, 20)
            v.wait_ge(kept, 1)
            nc.vector.scalar_tensor_tensor(by_expert[:, :], keep, tanh_g[:, 1:2], room,
                                           ALU.mult, ALU.mult).then_inc(fw_done, 1)

            def finish(n):
                v.wait_ge(weight_here, n * (16 * ST))
                v.wait_ge(ffn2_done, n * ST + 1)
                v.wait_ge(added, n * (16 * ST))
                nc.vector.tensor_scalar(y[:, 1, :], ffn2[:, 1, 0:D], y_weight[:, 1:2], None,
                                        ALU.mult).then_inc(y_done[1], 1)

            def see_tokens(loaded):
                v.wait_ge(rows_loaded, loaded)
                nc.vector.tensor_copy(next_token[:, :], e_rows[:, :, D]).then_inc(token_seen, 1)

            def chunk(g, follows):
                v.wait_ge(et_hi, g + 1)
                lo(et_l[:, :, :], e_turned[:, :, :], et_h[:, :, :]).then_inc(et_lo, 1)
                for c in range(FC):
                    v.wait_ge(silu_done, g * FC + c + 1)
                    nc.vector.tensor_tensor(act_f[:, c % 2, :], ffn1[:, c % 4, 0, :], silu[:, :], ALU.mult)\
                        .then_inc(act_done, 1)
                    v.wait_ge(act_hi, g * FC + c + 1)
                    lo(act_l[:, c, :], act_f[:, c % 2, :], act_h[:, c, :]).then_inc(act_lo, 1)
                    if c == 0 and follows:
                        finish(g)
                    if c == 4:
                        v.wait_ge(added, g * (16 * ST) + 16 * ST)
                        v.wait_ge(token_seen, g + 2)
                        nc.vector.tensor_copy(y_token[:, :], next_token[:, :]).then_inc(token_copied, 1)
                        v.wait_ge(token_copied, g + 1)
                        nc.vector.tensor_scalar(y_at[:, :], next_token[:, :], e_base[:, 0:1], None,
                                                ALU.add).then_inc(token_done, 1)
                    if c == 6:
                        see_tokens(g * 16 + 32)

            nc.vector.memset(e_base[:, :], 0.0).then_inc(base_done, 1)
            see_tokens(16)
            v.wait_ge(table_done, 1)
            with v.Fori(0, E) as e:
                chunks = v.value_load(table[0:1, 0, ds(e, 1)], min_val=2, max_val=T // CHUNK)
                before = v.value_load(table[0:1, 1, ds(e, 1)], min_val=0, max_val=MOST_CHUNKS)
                v.wait_ge(base_done, e + 1)
                chunk(v.snap(before + 0), False)
                with v.Fori(1, chunks) as j:
                    chunk(v.snap(before + j), True)
                finish(v.snap(before + chunks))
                nc.vector.tensor_scalar(e_base[:, :], e_base[:, :], float(ROWS), None, ALU.add)\
                    .then_inc(base_done, 1)


def kernel(x, ctx_1024, g_xattn, g_ffn, L0_xattn_Wq, L0_xattn_Wk, L0_xattn_Wv, L0_xattn_Wo,
           L0_xattn_bo, L0_ffn_router_weight, L0_ffn_ff_pre_act_weight, L0_ffn_gate_weight,
           L0_ffn_ff_post_act_weight):
    import numpy as np
    import concourse.bacc as bacc
    from concourse.bass_utils import run_bass_kernel_spmd

    def flat(a, rows):
        return np.ascontiguousarray(np.asarray(a)).reshape(rows, -1)

    def turned(a):
        return np.swapaxes(np.asarray(a), -1, -2)

    arrays = {
        "x": flat(x, T),
        "ctx_t": flat(turned(ctx_1024), B * D),
        "g_attn": np.asarray(g_xattn), "g_ffn": np.asarray(g_ffn),
        "wq": np.asarray(L0_xattn_Wq), "wk": np.asarray(L0_xattn_Wk), "wv": np.asarray(L0_xattn_Wv),
        "wo": np.asarray(L0_xattn_Wo), "bo": np.asarray(L0_xattn_bo),
        "rw_t": flat(turned(L0_ffn_router_weight), D),
        "w1_t": flat(turned(L0_ffn_ff_pre_act_weight), E * D),
        "wg_t": flat(turned(L0_ffn_gate_weight), E * D),
        "w2_t": flat(turned(L0_ffn_ff_post_act_weight), E * FF),
    }
    nc = bacc.Bacc("TRN2", target_bir_lowering=False, num_devices=1)
    args = {name: nc.dram_tensor(name, a.shape, mybir.dt.from_np(a.dtype), kind="ExternalInput").ap()
            for name, a in arrays.items()}
    out = nc.dram_tensor("out", (ROWS, D), F32, kind="ExternalOutput").ap()
    build(nc, out=out, **args)
    result = run_bass_kernel_spmd(nc, [arrays], core_ids=[0])
    return result.results[0]["out"][:T].reshape(B, N, D)
```

```python
from contextlib import ExitStack

import concourse.bass as bass
from concourse import mybir
from concourse.bass import ds

F32 = mybir.dt.float32
F32R = mybir.dt.float32r
BF16 = mybir.dt.bfloat16
I32 = mybir.dt.int32
U32 = mybir.dt.uint32
ALU = mybir.AluOpType
ACT = mybir.ActivationFunctionType
AX = mybir.AxisListType

P = 128
B, N, D = 8, 512, 256
M = 1024
H, DH = 8, 64
INNER = H * DH
T = B * N
KC = D // P
QT = N // P
KT = M // P
UNITS = H * QT
PAIRS = H // 2
SCALE = DH ** -0.5
LN_EPS = 1e-5

E = 8
GROUPS = P // E
GT = T // GROUPS
FF = 1024
FC = FF // P
EPS = 1.1920929e-07
CAPACITY = (T * 2 * 5 + 4 * E - 1) // (4 * E)
WEIGHT_BITS = 30
CHUNK = 256
ST = CHUNK // P
MOST_CHUNKS = 2 * T // CHUNK + 2 * E
PAD = 2 * CHUNK
ROWS = T + PAD
RW = D + 4

JOBS = {
    0: [("k", 1, 0), ("q", 1, 0)], 2: [("k", 1, 1), ("v", 0, 3)], 4: [("w", 1, 0), ("w", 1, 1)],
    6: [("w", 1, 2), ("w", 1, 3)], 8: [("v", 1, 0), ("q", 2, 0)], 10: [("v", 1, 1), ("k", 2, 0)],
    12: [("k", 2, 1), ("v", 1, 2)], 14: [("v", 1, 3), ("h", 0, 0)], 15: [("h", 1, 0)],
    16: [("q", 3, 0)], 17: [("l", 0, 0)], 18: [("k", 3, 0), ("k", 3, 1)],
    20: [("w", 0, 0), ("w", 0, 1)], 22: [("w", 0, 2), ("w", 0, 3)], 24: [("x", 0, 0), ("x", 1, 0)],
    25: [("r", 0, 0)], 26: [("q", 0, 0), ("v", 0, 0)], 28: [("v", 0, 1), ("k", 0, 0)],
    30: [("k", 0, 1), ("v", 0, 2)],
}
LN_STEPS = 6
GATE_STEPS = 27
RANK_STEPS = 5
CONSTS = 16
NEXT_FROM = 24
END_STEPS = 27


class Body:

    def __init__(self, b, prev, own, nxt, offset, before):
        self.b, self.prev, self.own, self.nxt, self.before = b, prev, own, nxt, before
        self.offset = offset
        self.steps, place = [], offset
        for u in range(UNITS if own or nxt else END_STEPS):
            mine = []
            if u % 2 == 1 and (prev if u < 5 else own):
                mine.append(("o", ((u - 5) % UNITS) // 2, 0))
            for job in JOBS.get(u, []):
                if job[0] in "hlr" or job[:2] == ("w", 1):
                    wanted = prev
                elif job[0] in "xqkv" and u >= NEXT_FROM:
                    wanted = nxt
                else:
                    wanted = own
                if wanted:
                    mine.append(job)
            self.steps.append([(job, place + i) for i, job in enumerate(mine)])
            place += len(mine)
        self.end = place
        self.where = {job: c for step in self.steps for job, c in step}

    def results(self, u):
        if u > 0:
            return self.steps[u - 1]
        return [(job, c - RING) for job, c in self.before.steps[-1]] if self.before else []

    def of(self, b):
        return Body(b, self.prev, self.own, self.nxt, self.offset, self.before)

    def place(self, job):
        if job[0] != "x" and (job[1] > 0 or job == ("v", 0, 3)):
            return self.where[job]
        return self.before.where[job] - RING


RING = Body(1, True, True, True, 0, None).end
START = Body(-1, False, False, True, RING, None)
FIRST = Body(0, False, True, True, START.end - RING, START)
MIDDLE = Body(1, True, True, True, FIRST.end - RING, None)
MIDDLE.before = MIDDLE
LAST = Body(B - 1, True, True, False, MIDDLE.end - RING, MIDDLE)
END = Body(B, True, False, False, LAST.end - RING, LAST)
assert RING % 2 == 0 and MIDDLE.end - RING == FIRST.end - RING


def at(b, per_batch, n):
    return b * per_batch + n


def until(eng, sem, value):
    if not isinstance(value, int) or value > 0:
        eng.wait_ge(sem, value)


def build(nc, x, ctx_t, g_attn, g_ffn, wq, wk, wv, wo, bo, rw_t, w1_t, wg_t, w2_t, out):
    lists = nc.dram_tensor("lists", (E * ROWS, RW), F32, kind="Internal").ap()
    weights_of = nc.dram_tensor("weights_of", (E * ROWS, 1), F32, kind="Internal").ap()

    with ExitStack() as ctx:
        def sem(name):
            return ctx.enter_context(nc.semaphore(name))

        def tile(where, name, shape, dt=F32):
            return where.enter_context(nc.sbuf_tensor(name, shape, dt))

        ident = tile(ctx, "ident", [P, P])
        tanh_g = tile(ctx, "tanh_g", [P, 2])
        assigned = tile(ctx, "assigned", [P, E, T // P])
        list_end = tile(ctx, "list_end", [P, E])
        expert_row = tile(ctx, "expert_row", [P, E])
        same_expert = tile(ctx, "same_expert", [P, P])
        before_it = tile(ctx, "before_it", [P, P])
        same_group = tile(ctx, "same_group", [P, P])

        attn = ExitStack()
        wq_h = tile(attn, "wq_h", [P, KC, INNER], F32R)
        wq_l = tile(attn, "wq_l", [P, KC, INNER], F32R)
        wk_h = tile(attn, "wk_h", [P, KC, INNER], F32R)
        wk_l = tile(attn, "wk_l", [P, KC, INNER], F32R)
        wv_h = tile(attn, "wv_h", [P, KC, INNER], F32R)
        wv_l = tile(attn, "wv_l", [P, KC, INNER], F32R)
        wo_h = tile(attn, "wo_h", [P, H, D], F32R)
        wo_l = tile(attn, "wo_l", [P, H, D], F32R)
        k_st = tile(attn, "k_st", [P, 2, 2, M], F32R)
        q_h = tile(attn, "q_h", [P, 2, 2, N], F32R)
        q_l = tile(attn, "q_l", [P, 2, 2, N], F32R)
        ctx_raw = tile(attn, "ctx_raw", [P, KC, M // 2])
        h_flat = ctx_raw[:, :, :].rearrange("p c m -> p (c m)")
        h_t = h_flat.rearrange("p (q c t) -> p q c t", c=KC, t=P)
        x_in = tile(attn, "x_in", [P, QT, D])
        x_sum = tile(attn, "x_sum", [P, QT, D])
        rows = tile(attn, "rows", [P, QT, RW])
        bias_o = tile(attn, "bias_o", [P, D])
        rw = tile(attn, "rw", [P, KC, E])
        ctx_h = tile(attn, "ctx_h", [P, KC, M], F32R)
        ctx_l = tile(attn, "ctx_l", [P, KC, M], F32R)
        xt_h = tile(attn, "xt_h", [P, KC, N], F32R)
        xt_l = tile(attn, "xt_l", [P, KC, N], F32R)
        v_hl = tile(attn, "v_hl", [P, KT, H, P], F32R)
        probs = tile(attn, "probs", [P, 2, M])
        pt_h = tile(attn, "pt_h", [P, 2, KT, 2 * P], F32R)
        pt_l = tile(attn, "pt_l", [P, 2, KT, 2 * P], F32R)
        ot_h = tile(attn, "ot_h", [P, H // 2, N], F32R)
        ot_l = tile(attn, "ot_l", [P, H // 2, N], F32R)
        neg_max = tile(attn, "neg_max", [P, 2])
        row_sum = tile(attn, "row_sum", [P, 2])
        row_rec = tile(attn, "row_rec", [P, 2])
        earlier = tile(attn, "earlier", [P, P], BF16)
        ones = tile(attn, "ones", [P, P], BF16)
        chosen = tile(attn, "chosen", [P, QT, E], BF16)
        stats = tile(attn, "stats", [P, 2, QT, 6])
        mean_var = tile(attn, "mean_var", [P, 2, QT, 2])
        norm = tile(attn, "norm", [P, 2, 6, QT])
        minus_half = tile(attn, "minus_half", [P, QT])
        rev = tile(attn, "rev", [P, E])
        token = tile(attn, "token", [P, QT])
        gate = tile(attn, "gate", [P, 8, QT, E])
        gate1 = tile(attn, "gate1", [P, 8, QT])
        quotient = tile(attn, "quotient", [P, 3, 2, QT])
        oh = tile(attn, "oh", [P, 2, QT, E])
        oh_x = tile(attn, "oh_x", [P, 2, QT, E])
        row_f = tile(attn, "row_f", [P, 2, QT])
        list_row = tile(attn, "list_row", [P, 2, QT], U32)
        attn.close()

        moe = ExitStack()
        w_raw = [tile(moe, f"{n}_raw", [P, KC * FF]) for n in ("w1", "wg", "w2")]
        w_parts = [[[tile(moe, f"{n}_{part}{i}", [P, KC * FF], F32R) for n in ("w1", "wg", "w2")]
                    for part in "hl"] for i in range(2)]
        w_h, w_l = [parts[0] for parts in w_parts], [parts[1] for parts in w_parts]
        e_rows = tile(moe, "e_rows", [P, ST, RW])
        et_h = tile(moe, "et_h", [P, KC, CHUNK], F32R)
        et_l = tile(moe, "et_l", [P, KC, CHUNK], F32R)
        silu = tile(moe, "silu", [P, CHUNK])
        act_f = tile(moe, "act_f", [P, 2, CHUNK])
        act_h = tile(moe, "act_h", [P, FC, CHUNK], F32R)
        act_l = tile(moe, "act_l", [P, FC, CHUNK], F32R)
        y = tile(moe, "y", [P, ST, D])
        pad_rows = tile(moe, "pad_rows", [P, ST, RW])
        zeros = tile(moe, "zeros", [P, PAD // P, D])
        y_weight = tile(moe, "y_weight", [P, ST])
        next_token = tile(moe, "next_token", [P, ST])
        y_token = tile(moe, "y_token", [P, ST], U32)
        y_at = tile(moe, "y_at", [P, ST], U32)
        e_base = tile(moe, "e_base", [P, 1])
        by_expert = tile(moe, "by_expert", [P, GT])
        work = tile(moe, "work", [P, 5, GT])
        threshold = tile(moe, "threshold", [P, 1], I32)
        candidate = tile(moe, "candidate", [P, 1], I32)
        raised = tile(moe, "raised", [P, 1], I32)
        bit = tile(moe, "bit", [P, 1], I32)
        bit_f = tile(moe, "bit_f", [P, 1])
        counts = tile(moe, "counts", [P, 4])
        table_f = tile(moe, "table_f", [P, 3, E])
        table = tile(moe, "table", [P, 4, E], I32)
        moe.close()

        banks = ExitStack()
        scores = banks.enter_context(nc.psum_tensor("scores", [P, 2, M], F32))
        turned = banks.enter_context(nc.psum_tensor("turned", [P, KT, P], F32))
        ring = banks.enter_context(nc.psum_tensor("ring", [P, 2, 512], F32))
        banks.close()
        banks = ExitStack()
        ffn1 = banks.enter_context(nc.psum_tensor("ffn1", [P, 4, 2, CHUNK], F32))
        e_turned = banks.enter_context(nc.psum_tensor("e_turned", [P, KC, CHUNK], F32))
        ffn2 = banks.enter_context(nc.psum_tensor("ffn2", [P, ST, 512], F32))
        misc = banks.enter_context(nc.psum_tensor("misc", [P, 512], F32))
        banks.close()

        x_loaded = sem("x_loaded")
        ctx_loaded = sem("ctx_loaded")
        sum_loaded = sem("sum_loaded")
        small_loaded = sem("small_loaded")
        raw_loaded = [sem(f"raw_loaded{i}") for i in range(5)]
        consts = sem("consts")
        waited = sem("waited")
        tanh_done = sem("tanh_done")
        bias_done = sem("bias_done")
        raw_hi = sem("raw_hi")
        weights_split = sem("weights_split")
        ctx_hi = sem("ctx_hi")
        ctx_split = sem("ctx_split")
        scores_done = sem("scores_done")
        neg_done = sem("neg_done")
        exp_done = sem("exp_done")
        rec_done = sem("rec_done")
        scaled = sem("scaled")
        turned_done = sem("turned_done")
        pt_hi = sem("pt_hi")
        pt_lo = sem("pt_lo")
        filled = sem("filled")
        drained = [sem("drained0"), sem("drained1")]
        hi_done = {k: sem(f"hi_{k}") for k in "qkvox"}
        hi_events = {"q": PAIRS, "k": H, "v": KT, "o": 2 * H, "x": KC}
        ln_seq = [sem("ln1_seq"), sem("ln2_seq")]
        var_done = [sem("var1_done"), sem("var2_done")]
        pow_done = [sem("pow1_done"), sem("pow2_done")]
        ln_ready = [sem("ln1_ready"), sem("ln2_ready")]
        normed = [sem("normed1"), sem("normed2")]
        biased = sem("biased")
        sum_stored = sem("sum_stored")
        gate_seq = sem("gate_seq")
        gate_exp = sem("gate_exp")
        chosen_done = sem("chosen_done")
        rank_seq = sem("rank_seq")
        list_row_done = sem("list_row_done")
        listed = sem("listed")
        more_done = sem("more_done")
        gathered = sem("gathered")
        search_seq = sem("search_seq")
        search_bits = sem("search_bits")
        counted = sem("counted")
        summed = sem("summed")
        masked = sem("masked")
        ranked = sem("ranked")
        kept = sem("kept")
        wsum_done = sem("wsum_done")
        table_done = sem("table_done")
        fw_done = sem("fw_done")
        fw_stored = sem("fw_stored")
        pads_ready = sem("pads_ready")
        pads_stored = sem("pads_stored")
        first_pads = sem("first_pads")
        w_loaded = [sem(f"w_loaded{i}") for i in range(3)]
        w_first_hi = sem("w_first_hi")
        w_hi = sem("w_hi")
        w_split = sem("w_split")
        rows_loaded = sem("rows_loaded")
        e_turned_done = sem("e_turned_done")
        et_hi = sem("et_hi")
        et_lo = sem("et_lo")
        ffn1_done = sem("ffn1_done")
        silu_done = sem("silu_done")
        act_done = sem("act_done")
        act_hi = sem("act_hi")
        act_lo = sem("act_lo")
        ffn2_done = sem("ffn2_done")
        y_done = [sem("y_done0"), sem("y_done1")]
        token_seen = sem("token_seen")
        token_copied = sem("token_copied")
        token_done = sem("token_done")
        base_done = sem("base_done")
        weight_here = sem("weight_here")
        added = sem("added")

        def alone(eng):
            eng.sem_inc(waited, 1)

        def wait_filled(eng, body, c):
            eng.wait_ge(filled, at(body.b, RING, c + 1))

        def wait_drained(eng, body, c):
            until(eng, drained[c % 2], at(body.b, RING // 2, c // 2 + 1))

        def wait_all_drained(eng, body, places):
            for bank in range(2):
                of_bank = [c for c in places if c % 2 == bank]
                if of_bank:
                    wait_drained(eng, body, max(of_bank))

        def batches(eng, run):
            run(START)
            run(FIRST)
            with eng.Fori(1, B - 1) as b:
                run(MIDDLE.of(b))
            run(LAST)
            run(END)

        def wait_hi(eng, kind, b, n):
            eng.wait_ge(hi_done[kind], at(b, hi_events[kind], n + 1))

        def of_batch(body, job, u):
            kind, i, j = job
            b = body.b
            if kind == "o":
                return (b - 1 if u < 5 else b), i
            if u >= NEXT_FROM:
                b = b + 1
            return b, {"q": i, "k": 2 * i + j, "v": 4 * i + j, "x": i}[kind]

        def load_w(eng, i, e):
            w = (w1_t, wg_t, w2_t)[i]
            k = w.shape[0] // E
            eng.dma_start(w_raw[i][:, :].rearrange("p (c n) -> p c n", c=k // P),
                          w[ds(e * k, k), :].rearrange("(c p) n -> p c n", p=P))\
                .then_inc(w_loaded[i], 16)

        def pad_lists(eng, half):
            eng.wait_ge(table_done, 1)
            with eng.Fori(half * E // 2, (half + 1) * E // 2) as e:
                n = eng.value_load(table[0:1, 2, ds(e, 1)], min_val=0, max_val=T)
                row = eng.snap(n + e * ROWS)
                eng.dma_start(lists[ds(row, CHUNK), :].rearrange("(q p) c -> p q c", p=P),
                              pad_rows[:, :, :]).then_inc(pads_stored, 16)

        block = ctx.enter_context(nc.Block())

        @block.sync
        def _(sp):
            def load_x(b, dst, s):
                sp.dma_start(dst[:, :, :], x[ds(b * N, N), :].rearrange("(q p) d -> p q d", p=P))\
                    .then_inc(s, 16)

            def load_ctx(b, half):
                src = ctx_t[ds(b * D, D), half * (M // 2):(half + 1) * (M // 2)]
                sp.dma_start(ctx_raw[:, :, :], src.rearrange("(c p) m -> p c m", p=P))\
                    .then_inc(ctx_loaded, 16)

            def store_sum(b):
                sp.dma_start(out[ds(b * N, N), :].rearrange("(q p) d -> p q d", p=P), x_sum[:, :, :])\
                    .then_inc(sum_stored, 16)

            def start():
                load_x(0, x_in, x_loaded)
                load_ctx(0, 0)
                for i, (w, dst) in enumerate(((wq, probs[:, 0, :]), (wk, probs[:, 1, :]),
                                              (wv, x_sum[:, :, :].rearrange("p q d -> p (q d)")))):
                    sp.dma_start(dst.rearrange("p (c n) -> p c n", c=KC),
                                 w.rearrange("(c p) n -> p c n", p=P)).then_inc(raw_loaded[i], 16)
                sp.dma_start(tanh_g[:, 0:1], g_attn.partition_broadcast(P)).then_inc(small_loaded, 16)
                sp.dma_start(tanh_g[:, 1:2], g_ffn.partition_broadcast(P)).then_inc(small_loaded, 16)
                sp.dma_start(bias_o[:, :], bo.partition_broadcast(P)).then_inc(small_loaded, 16)
                sp.dma_start(rw[:, :, :], rw_t.rearrange("(c p) e -> p c e", p=P))\
                    .then_inc(small_loaded, 16)
                sp.wait_ge(ctx_split, 1)
                load_ctx(0, 1)
                sp.wait_ge(consts, CONSTS)
                for e in range(E):
                    sp.dma_start(lists[e * ROWS + CHUNK:e * ROWS + PAD, :]
                                 .rearrange("(q p) c -> p q c", p=P), rows[:, 0:ST, :])\
                        .then_inc(first_pads, 16)

            def load_wo():
                for half in range(2):
                    sp.wait_ge(weights_split, 3 + half)
                    for copy_ in range(2):
                        sp.dma_start(x_sum[copy_ * DH:(copy_ + 1) * DH, :, :],
                                     wo[half * (INNER // 2):(half + 1) * (INNER // 2), :]
                                     .rearrange("(h p) d -> p h d", p=DH))\
                            .then_inc(raw_loaded[3 + half], 16)
                sp.wait_ge(weights_split, 5)

            def run(body):
                b = body.b
                if body is START:
                    start()
                    return
                if body.nxt:
                    wait_filled(sp, body, body.place(("v", 0, 0)))
                    alone(sp)
                    load_x(b + 1, x_in, x_loaded)
                if body.prev:
                    wait_drained(sp, body, body.where[("w", 1, 3)])
                    alone(sp)
                    store_sum(b - 1)
                if body.prev:
                    sp.wait_ge(sum_stored, at(b, 16, 0))
                    alone(sp)
                    sp.wait_ge(normed[1], at(b, QT, 0))
                    alone(sp)
                else:
                    load_wo()
                if body.own:
                    load_x(b, x_sum, sum_loaded)
                if body.nxt:
                    sp.wait_ge(ctx_split, at(b, 2, 2))
                    alone(sp)
                    if body.prev:
                        wait_filled(sp, body, body.where[("l", 0, 0)])
                        alone(sp)
                    load_ctx(b + 1, 0)
                    sp.wait_ge(ctx_split, at(b, 2, 3))
                    alone(sp)
                    load_ctx(b + 1, 1)
                elif body.own:
                    wait_filled(sp, body, body.where[("k", 3, 1)])
                    alone(sp)
                    for i in range(3):
                        load_w(sp, i, 0)

            batches(sp, run)

            sp.wait_ge(pads_ready, 3)
            sp.wait_ge(w_split, 3)
            for i in range(3):
                load_w(sp, i, 1)
            pad_lists(sp, 0)
            sp.wait_ge(pads_stored, 16 * E)

            def load_rows(row):
                sp.dma_start(e_rows[:, :, :],
                             lists[ds(row, CHUNK), :].rearrange("(q p) c -> p q c", p=P))\
                    .then_inc(rows_loaded, 16)

            sp.wait_ge(listed, 16 * 2 * QT * B)
            def expert(e, reload):
                chunks = sp.value_load(table[0:1, 0, ds(e, 1)], min_val=2, max_val=T // CHUNK)
                before = sp.value_load(table[0:1, 1, ds(e, 1)], min_val=0, max_val=MOST_CHUNKS)
                with sp.Fori(0, chunks) as j:
                    free = sp.snap(before + j + 1)
                    row = sp.snap(e * ROWS + j * CHUNK)
                    sp.wait_ge(e_turned_done, free)
                    sp.wait_ge(token_seen, free)
                    alone(sp)
                    load_rows(row)
                if reload:
                    for i in range(3):
                        sp.wait_ge(w_split, at(e, 3, 3 + i + 1))
                        alone(sp)
                        load_w(sp, i, e + 2)

            with sp.Fori(0, E - 2) as e:
                expert(e, True)
            with sp.Fori(E - 2, E) as e:
                expert(e, False)
            total = sp.value_load(table[0:1, 3, 0:1], min_val=2, max_val=MOST_CHUNKS)
            free = sp.snap(total + 1)
            all_added = sp.snap(total * (16 * ST) + 16 * ST)
            sp.wait_ge(e_turned_done, free)
            sp.wait_ge(token_seen, free)
            alone(sp)
            load_rows(0)
            sp.wait_ge(rows_loaded, 16)
            sp.wait_ge(added, all_added)
            alone(sp)

        @block.gpsimd
        def _(pool):
            def const(ins):
                ins.then_inc(consts, 1)

            const(nc.gpsimd.memset(minus_half[:, :], -0.5))
            const(nc.gpsimd.memset(ident[:, :], 1.0))
            const(nc.gpsimd.memset(same_expert[:, :], 1.0))
            const(nc.gpsimd.memset(earlier[:, :], 1.0))
            const(nc.gpsimd.memset(ones[:, :], 1.0))
            const(nc.gpsimd.memset(same_group[:, :], 0.0))
            const(nc.gpsimd.memset(rows[:, :, :], 0.0))
            const(nc.gpsimd.iota(rev[:, :], [[-1, E]], base=E, channel_multiplier=0,
                                 allow_small_or_imprecise_dtypes=True))
            const(nc.gpsimd.iota(token[:, :], [[P, QT]], base=0, channel_multiplier=1,
                                 allow_small_or_imprecise_dtypes=True))
            const(nc.gpsimd.iota(expert_row[:, :], [[ROWS, E]], base=0, channel_multiplier=0,
                                 allow_small_or_imprecise_dtypes=True))
            const(nc.gpsimd.iota(list_end[:, :], [[ROWS, E]], base=0, channel_multiplier=0,
                                 allow_small_or_imprecise_dtypes=True))
            pool.wait_ge(consts, 7)
            const(nc.gpsimd.iota(rows[:, 0:ST, D:D + 1], [[P, ST], [0, 1]], base=T + CHUNK,
                                 channel_multiplier=1, allow_small_or_imprecise_dtypes=True))
            const(nc.gpsimd.affine_select(out=ident[:, :], in_=ident[:, :], compare_op=ALU.is_equal,
                                          fill=0.0, base=0, pattern=[[-1, P]], channel_multiplier=1))
            const(nc.gpsimd.affine_select(out=earlier[:, :], in_=earlier[:, :],
                                          compare_op=ALU.is_gt, fill=0.0, base=0, pattern=[[1, P]],
                                          channel_multiplier=-1))
            grid = same_expert[:, :].rearrange("p (e c) -> p e c", e=E)
            const(nc.gpsimd.affine_select(out=grid, in_=grid, compare_op=ALU.is_ge, fill=0.0, base=0,
                                          pattern=[[-GROUPS, E], [0, GROUPS]], channel_multiplier=1))
            pool.wait_ge(consts, 15)
            const(nc.gpsimd.affine_select(out=grid, in_=grid, compare_op=ALU.is_ge, fill=0.0,
                                          base=GROUPS - 1, pattern=[[GROUPS, E], [0, GROUPS]],
                                          channel_multiplier=-1))

            def more_consts():
                nc.gpsimd.affine_select(out=before_it[:, :], in_=same_expert[:, :],
                                        compare_op=ALU.is_gt, fill=0.0, base=0, pattern=[[1, P]],
                                        channel_multiplier=-1).then_inc(more_done, 1)
                group = same_group[:, :].rearrange("p (e c) -> p e c", e=E)
                for k in range(E):
                    pool.wait_ge(more_done, 1 + k)
                    nc.gpsimd.affine_select(out=group, in_=group, compare_op=ALU.not_equal, fill=1.0,
                                            base=-GROUPS * k, pattern=[[0, E], [-1, GROUPS]],
                                            channel_multiplier=1).then_inc(more_done, 1)

            def split_ctx(b, half):
                part = slice(half * (M // 2), (half + 1) * (M // 2))
                pool.wait_ge(ctx_loaded, at(b, 32, 16 * (half + 1)))
                alone(pool)
                nc.gpsimd.tensor_scalar(ctx_h[:, :, part], ctx_raw[:, :, :], 1.0, 1.0,
                                        ALU.mult, ALU.mult).then_inc(ctx_hi, 1)
                pool.wait_ge(ctx_hi, at(b, 2, half + 1))
                nc.gpsimd.tensor_tensor(ctx_l[:, :, part], ctx_raw[:, :, :],
                                        ctx_h[:, :, part].bitcast(F32), ALU.subtract)\
                    .then_inc(ctx_split, 1)

            def make_pads():
                nc.gpsimd.memset(zeros[:, :, :], 0.0).then_inc(pads_ready, 1)
                nc.gpsimd.memset(pad_rows[:, :, :], 0.0).then_inc(pads_ready, 1)
                pool.wait_ge(pads_ready, 2)
                nc.gpsimd.iota(pad_rows[:, :, D:D + 1], [[P, ST], [0, 1]], base=T,
                               channel_multiplier=1, allow_small_or_imprecise_dtypes=True)\
                    .then_inc(pads_ready, 1)

            def power(which, b):
                pool.wait_ge(var_done[which], at(b, 1, 1))
                nc.gpsimd.tensor_tensor(norm[:, which, 1, :], norm[:, which, 0, :], minus_half[:, :],
                                        ALU.pow).then_inc(pow_done[which], 1)

            def normalise(which, b, src, dst):
                pool.wait_ge(ln_ready[which], at(b, 1, 1))
                alone(pool)
                for q in range(QT):
                    nc.gpsimd.tensor_scalar(dst[:, q, 0:D], src[:, q, :],
                                            norm[:, which, 4, q:q + 1], norm[:, which, 5, q:q + 1],
                                            ALU.mult, ALU.add).then_inc(normed[which], 1)

            def scatter(b, i):
                q, k = i // 2, i % 2
                if i == 0:
                    pool.wait_ge(list_row_done, at(b, 1, 1))
                    alone(pool)
                nc.gpsimd.indirect_dma_start(
                    lists[:, :], bass.IndirectOffsetOnAxis(ap=list_row[:, k, q:q + 1], axis=0),
                    rows[:, q, :], None).then_inc(listed, 16)

            def run(body):
                b = body.b
                for u in range(len(body.steps)):
                    if body.own if u > 1 else body.prev:
                        k = u % 2
                        pool.wait_ge(rec_done, at(b, UNITS, u - 1))
                        alone(pool)
                        nc.gpsimd.tensor_scalar(probs[:, k, :], probs[:, k, :], row_rec[:, k:k + 1],
                                                1.0, ALU.mult, ALU.mult).then_inc(scaled, 1)
                    if body is FIRST and u == 3:
                        more_consts()
                    if body is END and u == 13:
                        make_pads()
                    if body.prev:
                        if u == 9:
                            power(1, b - 1)
                        if u == 12:
                            pool.wait_ge(first_pads, 16 * E)
                            normalise(1, b - 1, x_sum, rows)
                        if body.own and 27 <= u < 27 + QT:
                            for k in range(2):
                                scatter(b - 1, 2 * (u - 27) + k)
                        if u == UNITS - 1:
                            pool.wait_ge(listed, at(b - 1, 16 * 2 * QT, 16 * 2 * QT))
                            alone(pool)
                    if body.own and u == 15:
                        pool.wait_ge(sum_loaded, at(b, 16, 16))
                        pool.wait_ge(bias_done, 1)
                        nc.gpsimd.tensor_tensor(
                            x_sum[:, :, :], x_sum[:, :, :],
                            bias_o[:, :].unsqueeze(1).to_broadcast([P, QT, D]), ALU.add)\
                            .then_inc(biased, 1)
                    if body.nxt:
                        if u == 14:
                            power(0, b + 1)
                        if u == 17:
                            normalise(0, b + 1, x_in, x_in)
                        if u == 20:
                            if body.own:
                                wait_filled(pool, body, body.where[("k", 3, 1)])
                            split_ctx(b + 1, 0)
                        if u == 23:
                            split_ctx(b + 1, 1)
                if body is END:
                    for i in range(2 * QT):
                        scatter(b - 1, i)

            batches(pool, run)

            def split_w(e, i, parity):
                pool.wait_ge(w_loaded[i], at(e, 16, 16))
                alone(pool)
                nc.gpsimd.tensor_scalar(w_h[parity][i][:, :], w_raw[i][:, :], 1.0, 1.0,
                                        ALU.mult, ALU.mult).then_inc(w_hi, 1)
                pool.wait_ge(w_hi, at(e - 1, 3, i + 1))
                nc.gpsimd.tensor_tensor(w_l[parity][i][:, :], w_raw[i][:, :],
                                        w_h[parity][i][:, :].bitcast(F32), ALU.subtract)\
                    .then_inc(w_split, 1)

            pool.wait_ge(listed, 16 * 2 * QT * B)
            pool.wait_ge(sum_stored, 16 * B)
            pool.wait_ge(pads_ready, 3)
            nc.gpsimd.dma_start(out[T:ROWS, :].rearrange("(q p) d -> p q d", p=P), zeros[:, :, :])\
                .then_inc(added, 16)
            nc.gpsimd.dma_start(weights_of.rearrange("(e t) o -> e (t o)", e=E)[:, T:ROWS],
                                zeros[0:E, 0:PAD // D, :].rearrange("p q d -> p (q d)"))\
                .then_inc(added, 16)
            pool.wait_ge(added, 16 * ST)
            pool.wait_ge(fw_stored, 16 * E)
            pool.wait_ge(pads_stored, 16 * E)

            def gather(g):
                pool.wait_ge(token_done, g + 1)
                alone(pool)
                for st in range(ST):
                    nc.gpsimd.indirect_dma_start(
                        y_weight[:, st:st + 1], None, weights_of[:, :],
                        bass.IndirectOffsetOnAxis(ap=y_at[:, st:st + 1], axis=0))\
                        .then_inc(weight_here, 16)

            def scatter_add(g):
                pool.wait_ge(added, g * (16 * ST) + 16 * ST)
                for st in range(ST):
                    pool.wait_ge(y_done[st], g + 2)
                    alone(pool)
                    nc.gpsimd.indirect_dma_start(
                        out[:, :], bass.IndirectOffsetOnAxis(ap=y_token[:, st:st + 1], axis=0),
                        y[:, st, :], None, compute_op=ALU.add).then_inc(added, 16)

            def expert(e, parity, has_next):
                chunks = pool.value_load(table[0:1, 0, ds(e, 1)], min_val=2, max_val=T // CHUNK)
                before = pool.value_load(table[0:1, 1, ds(e, 1)], min_val=0,
                                         max_val=MOST_CHUNKS)
                first = pool.snap(before + 0)
                if has_next:
                    split_w(e + 1, 0, 1 - parity)
                gather(first)
                if has_next:
                    split_w(e + 1, 1, 1 - parity)
                scatter_add(first)
                if has_next:
                    split_w(e + 1, 2, 1 - parity)
                with pool.Fori(1, chunks) as j:
                    g = pool.snap(before + j)
                    gather(g)
                    scatter_add(g)

            pool.wait_ge(table_done, 1)
            expert(0, 0, True)
            expert(1, 1, True)
            with pool.Fori(1, E // 2 - 1) as pair:
                for parity in range(2):
                    expert(2 * pair + parity, parity, True)
            for parity in range(2):
                expert(E - 2 + parity, parity, parity == 0)

        def passes(out_, st, mv, start, stop):
            (sh, sl), (mh, ml) = st, mv
            nc.tensor.matmul(out_, sh, mh, start=start, stop=False)
            nc.tensor.matmul(out_, sh, ml, start=False, stop=False)
            return nc.tensor.matmul(out_, sl, mh, start=False, stop=stop)

        @block.tensor
        def _(pe):
            pe.sem_inc(e_turned_done, 1)
            pe.sem_inc(ffn1_done, 1)
            pe.sem_inc(ffn2_done, 1)

            def make_scores(body, u):
                b, h, q = body.b, u // QT, u % QT
                buf, ab = (h // 2) % 2, h % 2
                if u % (2 * QT) == 0:
                    wait_all_drained(pe, body, [body.place(("q", h // 2, 0))] +
                                     [body.place(("k", h // 2, keys)) for keys in range(2)])
                until(pe, exp_done, at(b, UNITS, u - 1))
                for part in (q_h, q_l):
                    for half in range(2):
                        cols = slice(half * 512, (half + 1) * 512)
                        last = nc.tensor.matmul(scores[:, u % 2, cols],
                                                part[:, buf, ab, q * P:(q + 1) * P],
                                                k_st[:, buf, ab, cols],
                                                start=part is q_h, stop=part is q_l)
                last.then_inc(scores_done, 1)

            def turn(body, n):
                pe.wait_ge(scaled, at(body.b, UNITS, n + 1))
                for j in range(2):
                    until(pe, pt_lo, at(body.b, 2 * UNITS, 2 * n - 1 + j))
                    for kt in range(4 * j, 4 * j + 4):
                        last = nc.tensor.transpose(turned[:, kt, :],
                                                   probs[:, n % 2, kt * P:(kt + 1) * P], ident[:, :])
                    last.then_inc(turned_done, 1)

            def wait_for_job(body, u, what):
                kind, i, j = what
                b = body.b
                reads = []
                if kind == "o":
                    m = i - 2 * H if u < 5 else i
                    pe.wait_ge(pt_lo, at(b, 2 * UNITS, 4 * m + 4))
                    if i % H == 0:
                        reads = [body.place(("v", i // H, keys)) for keys in range(4)]
                if kind == "w":
                    if body is FIRST and j == 0:
                        pe.wait_ge(weights_split, 5)
                    reads = [body.where[("o", H * i + H - 2 + j // 2, 0)]]
                if kind == "x":
                    pe.wait_ge(normed[0], at(b + 1, QT, QT))
                if what in (("v", 0, 0), ("k", 0, 1)):
                    pe.wait_ge(ctx_split, at(b + 1, 2, 1 + j))
                    if body is START and kind == "v":
                        pe.wait_ge(weights_split, 3)
                if kind == "q" and i == 0:
                    reads = [body.where[("x", 0, 0)], body.where[("x", 1, 0)]]
                    if body is START:
                        pe.wait_ge(weights_split, 1)
                if kind == "h":
                    pe.wait_ge(normed[1], at(b - 1, QT, 2 * i + 2))
                if kind == "l":
                    reads = [body.where[("h", 0, 0)], body.where[("h", 1, 0)]]
                if kind == "r":
                    pe.wait_ge(chosen_done, at(b - 1, 1, 1))
                return reads

            def do_job(what, bank):
                kind, i, j = what
                if kind == "q":
                    cols = slice(i * P, (i + 1) * P)
                    for kc in range(KC):
                        last = passes(bank, (wq_h[:, kc, cols], wq_l[:, kc, cols]),
                                      (xt_h[:, kc, :], xt_l[:, kc, :]), kc == 0, kc == KC - 1)
                if kind == "k":
                    cols, keys = slice(i * P, (i + 1) * P), slice(j * 512, (j + 1) * 512)
                    for kc in range(KC):
                        last = passes(bank, (wk_h[:, kc, cols], wk_l[:, kc, cols]),
                                      (ctx_h[:, kc, keys], ctx_l[:, kc, keys]), kc == 0, kc == KC - 1)
                if kind == "v":
                    cols = slice(i * 256, (i + 1) * 256)
                    for t in range(2):
                        keys = slice((2 * j + t) * P, (2 * j + t + 1) * P)
                        for kc in range(KC):
                            last = passes(bank[:, t * 256:(t + 1) * 256],
                                          (ctx_h[:, kc, keys], ctx_l[:, kc, keys]),
                                          (wv_h[:, kc, cols], wv_l[:, kc, cols]), kc == 0, kc == KC - 1)
                if kind == "w":
                    toks = slice(j * P, (j + 1) * P)
                    for h in range(H // 2):
                        head = i * (H // 2) + h
                        last = passes(bank[:, 0:D], (ot_h[:, h, toks], ot_l[:, h, toks]),
                                      (wo_h[:, head, :], wo_l[:, head, :]), h == 0, h == H // 2 - 1)
                if kind == "x":
                    for q in range(QT):
                        last = nc.tensor.transpose(bank[:, q * P:(q + 1) * P],
                                                   x_in[:, q, i * P:(i + 1) * P], ident[:, :])
                if kind == "h":
                    for t in range(2):
                        for kc in range(KC):
                            last = nc.tensor.transpose(
                                bank[:, (t * KC + kc) * P:(t * KC + kc + 1) * P],
                                rows[:, 2 * i + t, kc * P:(kc + 1) * P], ident[:, :])
                if kind == "l":
                    for q in range(QT):
                        for kc in range(KC):
                            last = nc.tensor.matmul(bank[:, q * E:(q + 1) * E], h_t[:, q, kc, :],
                                                    rw[:, kc, :], start=kc == 0, stop=kc == KC - 1)
                if kind == "r":
                    for q in range(QT):
                        nc.tensor.matmul(bank[:, q * E:(q + 1) * E], earlier[:, :], chosen[:, q, :],
                                         start=True, stop=q == 0)
                        for before in range(q):
                            nc.tensor.matmul(bank[:, q * E:(q + 1) * E], ones[:, :],
                                             chosen[:, before, :], start=False, stop=before == q - 1)
                    for q in range(QT):
                        last = nc.tensor.matmul(bank[:, QT * E:(QT + 1) * E], ones[:, :],
                                                chosen[:, q, :], start=q == 0, stop=q == QT - 1)
                if kind == "o":
                    h, m = i // 2, i % 2
                    for kt in range(KT):
                        for part in (pt_h, pt_l):
                            last = nc.tensor.matmul(bank[:, 0:2 * P], v_hl[:, kt, h, :],
                                                    part[:, m, kt, :],
                                                    start=kt == 0 and part is pt_h,
                                                    stop=kt == KT - 1 and part is pt_l)
                last.then_inc(filled, 1)

            def run(body):
                for u, jobs in enumerate(body.steps):
                    if body.own:
                        make_scores(body, u)
                    for what, c in jobs:
                        reads = wait_for_job(body, u, what)
                        wait_all_drained(pe, body, reads + [c - 2])
                        do_job(what, ring[:, c % 2, :])
                    if body.prev if u < 2 else body.own:
                        turn(body, u - 2)

            pe.wait_ge(consts, CONSTS)
            pe.wait_ge(small_loaded, 64)
            batches(pe, run)

            pe.wait_ge(list_row_done, B)
            for half in range(2):
                last = nc.tensor.transpose(misc[:, half * P:(half + 1) * P],
                                           assigned[:, :, half::2], ident[:, :])
            last.then_inc(gathered, 1)
            pe.wait_ge(more_done, E + 1)
            pe.wait_ge(table_done, 1)
            turns = pe.value_load(table[0:1, 3, 1:2], min_val=1, max_val=WEIGHT_BITS)
            with pe.Fori(0, turns) as i:
                pe.wait_ge(counted, i + 1)
                nc.tensor.matmul(misc[:, 0:1], same_expert[:, :], counts[:, 0:1],
                                 start=True, stop=True).then_inc(summed, 1)
            pe.wait_ge(masked, 1)
            nc.tensor.matmul(misc[:, 0:1], same_expert[:, :], counts[:, 1:2], start=True, stop=True)
            nc.tensor.matmul(misc[:, 1:2], before_it[:, :], counts[:, 2:3], start=True, stop=True)\
                .then_inc(ranked, 1)
            pe.wait_ge(kept, 1)
            nc.tensor.matmul(misc[:, GT:2 * GT], same_group[:, :], work[:, 3, :],
                             start=True, stop=True).then_inc(wsum_done, 1)

            def turn_rows(loaded):
                pe.wait_ge(rows_loaded, loaded)
                for kc in range(KC):
                    for st in range(ST):
                        last = nc.tensor.transpose(e_turned[:, kc, st * P:(st + 1) * P],
                                                   e_rows[:, st, kc * P:(kc + 1) * P], ident[:, :])
                last.then_inc(e_turned_done, 1)

            def up(g, c, parity):
                pe.wait_ge(act_done, g * FC + c + 1)
                for i in range(2):
                    for kc in range(KC):
                        cols = slice(kc * FF + c * P, kc * FF + (c + 1) * P)
                        last = passes(ffn1[:, c % 4, i, :],
                                      (w_h[parity][i][:, cols], w_l[parity][i][:, cols]),
                                      (et_h[:, kc, :], et_l[:, kc, :]), kc == 0, kc == KC - 1)
                last.then_inc(ffn1_done, 1)

            def down(g, c, parity):
                pe.wait_ge(act_lo, g * FC + c + 1)
                for st in range(ST):
                    if c == 0:
                        pe.wait_ge(y_done[st], g + 1)
                    toks, cols = slice(st * P, (st + 1) * P), slice(c * D, (c + 1) * D)
                    last = passes(ffn2[:, st, 0:D], (act_h[:, c, toks], act_l[:, c, toks]),
                                  (w_h[parity][2][:, cols], w_l[parity][2][:, cols]),
                                  c == 0, c == FC - 1)
                    if c == FC - 1:
                        last.then_inc(ffn2_done, 1)

            def chunk(g, parity, follows):
                pe.wait_ge(et_lo, g + 1)
                for c in range(FC):
                    up(g, c, parity)
                    if c == 0 and follows:
                        down(g - 1, FC - 1, parity)
                    if c == FC - 2:
                        turn_rows(g * 16 + 32)
                    if c >= 2:
                        down(g, c - 2, parity)
                down(g, FC - 2, parity)

            turn_rows(16)
            with pe.Fori(0, E // 2) as pair:
                for parity in range(2):
                    e = 2 * pair + parity
                    chunks = pe.value_load(table[0:1, 0, ds(e, 1)], min_val=2, max_val=T // CHUNK)
                    before = pe.value_load(table[0:1, 1, ds(e, 1)], min_val=0, max_val=MOST_CHUNKS)
                    pe.wait_ge(w_split, at(e, 3, 3))
                    chunk(pe.snap(before + 0), parity, False)
                    with pe.Fori(1, chunks) as j:
                        chunk(pe.snap(before + j), parity, True)
                    down(pe.snap(before + chunks - 1), FC - 1, parity)

        @block.scalar
        def _(act):
            act.sem_inc(y_done[0], 1)

            def hi(dst, src):
                return nc.scalar.activation(dst, src, ACT.Copy)

            def split_raw(i, raw, dst, loads):
                act.wait_ge(raw_loaded[i], 16 * loads)
                hi(dst, raw).then_inc(raw_hi, 1)

            def drain(body, u, what, c):
                kind, i, j = what
                if kind in "lrw":
                    return
                bank = ring[:, c % 2, :]
                wait_filled(act, body, c)
                if kind == "h":
                    hi(h_flat[:, i * 512:(i + 1) * 512], bank)\
                        .then_inc(drained[c % 2], 1)
                    return
                if kind == "q":
                    for ab in range(2):
                        for half in range(2):
                            last = nc.scalar.activation(q_h[half * DH:(half + 1) * DH, i % 2, ab, :],
                                                        bank[ab * DH:(ab + 1) * DH, :], ACT.Copy,
                                                        scale=SCALE)
                if kind == "k":
                    for ab in range(2):
                        head = slice(ab * DH, (ab + 1) * DH)
                        last = hi(k_st[head, i % 2, ab, j * 512:(j + 1) * 512], bank[head, :])
                if kind == "v":
                    last = hi(v_hl[:, 2 * j:2 * j + 2, 4 * i:4 * i + 4, 0:DH],
                              bank.rearrange("p (t h d) -> p t h d", t=2, d=DH))
                if kind == "o":
                    toks = slice((i % 2) * 2 * P, (i % 2 + 1) * 2 * P)
                    last = hi(ot_h[:, (i // 2) % 4, toks], bank[:, 0:2 * P])
                if kind == "x":
                    last = hi(xt_h[:, i, :], bank)
                last.then_inc(hi_done[kind], 1)

            def run(body):
                b = body.b
                for u in range(len(body.steps)):
                    jobs = body.results(u)
                    for what, c in jobs[:1]:
                        drain(body, u - 1, what, c)
                    if body.prev if u < 3 else body.own:
                        n = u - 3
                        toks = slice((n % 2) * P, (n % 2 + 1) * P)
                        for j in range(2):
                            act.wait_ge(turned_done, at(b, 2 * UNITS, 2 * n + j + 1))
                            keys = slice(4 * j, 4 * j + 4)
                            hi(pt_h[:, (n // 2) % 2, keys, toks], turned[:, keys, :])\
                                .then_inc(pt_hi, 1)
                    if body.prev and u == 19:
                        wait_drained(act, body, body.where[("l", 0, 0)])
                        nc.scalar.activation(gate[:, 1, :, :], gate[:, 0, :, :], ACT.Exp)\
                            .then_inc(gate_exp, 1)
                    for what, c in jobs[1:]:
                        drain(body, u - 1, what, c)
                    if body is END and u == 8:
                        wait_filled(act, body, body.where[("w", 1, 3)])
                        for i in range(3):
                            act.wait_ge(w_loaded[i], 16)
                            hi(w_h[0][i][:, :], w_raw[i][:, :]).then_inc(w_first_hi, 1)
                    if body is START and u in (19, 25):
                        flat = x_sum[:, :, :].rearrange("p q d -> p (q d)")
                        parts = (wq_h, probs[:, 0, :]), (wk_h, probs[:, 1, :]), (wv_h, flat)
                        for i in ((0,) if u == 19 else (1, 2)):
                            dst, raw = parts[i]
                            split_raw(i, raw, dst[:, :, :].rearrange("p c n -> p (c n)"), 1)
                    if body is FIRST and u in (5, 8):
                        half = (u - 5) // 3
                        split_raw(3 + half, x_sum[:, :, :], wo_h[:, half * 4:half * 4 + 4, :], 2)
                    if body.own if u > 0 else body.prev:
                        k = (u - 1) % 2
                        act.wait_ge(neg_done, at(b, UNITS, u))
                        nc.scalar.activation(probs[:, k, :], scores[:, k, :], ACT.Exp,
                                             bias=neg_max[:, k:k + 1],
                                             accum_out=row_sum[:, k:k + 1])\
                            .then_inc(exp_done, 1)

            act.wait_ge(small_loaded, 64)
            nc.scalar.activation(tanh_g[:, :], tanh_g[:, :], ACT.Tanh).then_inc(tanh_done, 1)
            batches(act, run)

            act.wait_ge(pads_ready, 3)
            pad_lists(act, 1)
            act.wait_ge(fw_done, 1)
            for e in range(E):
                act.dma_start(weights_of[e * ROWS:e * ROWS + T, :]
                              .rearrange("(c k) o -> c (k o)", k=GT),
                              by_expert[e * GROUPS:(e + 1) * GROUPS, :]).then_inc(fw_stored, 16)

            def finish(n):
                act.wait_ge(weight_here, n * (16 * ST))
                act.wait_ge(ffn2_done, n * ST)
                act.wait_ge(added, n * (16 * ST))
                nc.scalar.activation(y[:, 0, :], ffn2[:, 0, 0:D], ACT.Copy,
                                     scale=y_weight[:, 0:1]).then_inc(y_done[0], 1)

            def chunk(g, follows):
                for c in range(FC):
                    act.wait_ge(ffn1_done, g * FC + c + 2)
                    nc.scalar.activation(silu[:, :], ffn1[:, c % 4, 1, :], ACT.Silu)\
                        .then_inc(silu_done, 1)
                    if c == FC - 1:
                        act.wait_ge(e_turned_done, g + 3)
                        hi(et_h[:, :, :], e_turned[:, :, :]).then_inc(et_hi, 1)
                    act.wait_ge(act_done, g * FC + c + 5)
                    hi(act_h[:, c, :], act_f[:, c % 2, :]).then_inc(act_hi, 1)
                    if c == 0 and follows:
                        finish(g)

            act.wait_ge(e_turned_done, 2)
            hi(et_h[:, :, :], e_turned[:, :, :]).then_inc(et_hi, 1)
            act.wait_ge(table_done, 1)
            with act.Fori(0, E) as e:
                chunks = act.value_load(table[0:1, 0, ds(e, 1)], min_val=2, max_val=T // CHUNK)
                before = act.value_load(table[0:1, 1, ds(e, 1)], min_val=0, max_val=MOST_CHUNKS)
                chunk(act.snap(before + 0), False)
                with act.Fori(1, chunks) as j:
                    chunk(act.snap(before + j), True)
                finish(act.snap(before + chunks))

        @block.vector
        def _(v):
            v.sem_inc(y_done[1], 1)
            v.sem_inc(token_seen, 1)
            v.sem_inc(act_done, 4)

            def lo(dst, src, hi_part):
                return nc.vector.tensor_tensor(dst, src, hi_part.bitcast(F32), ALU.subtract)

            def split_raw(i, raw, dst, hi_part):
                v.wait_ge(raw_hi, i + 1)
                lo(dst, raw, hi_part).then_inc(weights_split, 1)

            def layer(which, b, src, part):
                var, y0, w0, w1, scale, shift = (norm[:, which, k, :] for k in range(6))

                def after(n):
                    v.wait_ge(ln_seq[which], at(b, LN_STEPS, n))

                if part in (0, 1):
                    for q in (2 * part, 2 * part + 1):
                        last = nc.vector.bn_stats(stats[:, which, q, :], src[:, q, :])
                    last.then_inc(ln_seq[which], 1)
                if part == 2:
                    after(2)
                    alone(v)
                    for q in range(QT):
                        last = nc.vector.bn_aggr(mean_var[:, which, q, :], stats[:, which, q, :])
                    last.then_inc(ln_seq[which], 1)
                if part == 3:
                    after(3)
                    nc.vector.tensor_scalar(var, mean_var[:, which, :, 1], LN_EPS, None, ALU.add)\
                        .then_inc(var_done[which], 1)
                if part == 4:
                    v.wait_ge(pow_done[which], at(b, 1, 1))
                    nc.vector.scalar_tensor_tensor(w0, y0, -0.5, y0, ALU.mult, ALU.mult)\
                        .then_inc(ln_seq[which], 1)
                if part == 5:
                    after(4)
                    nc.vector.tensor_tensor(w1, w0, var, ALU.mult).then_inc(ln_seq[which], 1)
                if part == 6:
                    after(5)
                    nc.vector.scalar_tensor_tensor(scale, w1, 1.5, y0, ALU.add, ALU.mult)\
                        .then_inc(ln_seq[which], 1)
                if part == 7:
                    after(6)
                    nc.vector.scalar_tensor_tensor(shift, mean_var[:, which, :, 0], -1.0, scale,
                                                   ALU.mult, ALU.mult).then_inc(ln_ready[which], 1)

            def route(b, part):
                def step(ins):
                    ins.then_inc(gate_seq, 1)

                def wide(t):
                    return t.unsqueeze(2).to_broadcast([P, QT, E])

                def twice(t):
                    return t.unsqueeze(1).to_broadcast([P, 2, QT])

                ranks = rev[:, :].unsqueeze(1).to_broadcast([P, QT, E])
                expd, prob, equal, others, mask, some = (gate[:, k, :, :] for k in range(1, 7))
                if part == 2:
                    v.wait_ge(gate_exp, at(b, 1, 1))
                else:
                    v.wait_ge(gate_seq, at(b, GATE_STEPS, part - 1))
                if part == 2:
                    step(nc.vector.reduce_sum(gate1[:, 3, :], expd, AX.X))
                if part == 3:
                    step(nc.vector.reciprocal(gate1[:, 4, :], gate1[:, 3, :]))
                if part == 4:
                    step(nc.vector.tensor_tensor(prob, expd, wide(gate1[:, 4, :]), ALU.mult))
                k, of = (0, prob) if part < 10 else (1, others)
                if part in (5, 11):
                    step(nc.vector.reduce_max(gate1[:, k, :], of, AX.X))
                if part in (6, 12):
                    step(nc.vector.tensor_tensor(equal, of, wide(gate1[:, k, :]), ALU.is_equal))
                if part in (7, 13):
                    step(nc.vector.tensor_tensor(some, equal, ranks, ALU.mult))
                if part in (8, 14):
                    step(nc.vector.reduce_max(gate1[:, 5, :], some, AX.X))
                if part in (9, 15):
                    step(nc.vector.tensor_tensor(oh[:, k, :, :], ranks, wide(gate1[:, 5, :]),
                                                 ALU.is_equal))
                if part == 10:
                    step(nc.vector.scalar_tensor_tensor(others, oh[:, 0, :, :], -2.0, prob,
                                                        ALU.mult, ALU.add))
                if part == 16:
                    nc.vector.tensor_tensor(chosen[:, :, :], oh[:, 0, :, :], oh[:, 1, :, :], ALU.add)\
                        .then_inc(chosen_done, 1)
                    step(nc.vector.scalar_tensor_tensor(mask, oh[:, 0, :, :], -1.0, oh[:, 1, :, :],
                                                        ALU.add, ALU.add))
                if part == 17:
                    step(nc.vector.tensor_tensor(gate1[:, 6, :], gate1[:, 0, :], gate1[:, 1, :],
                                                 ALU.add))
                if part == 18:
                    step(nc.vector.tensor_scalar(gate1[:, 7, :], gate1[:, 6, :], EPS, None, ALU.max))
                if part == 19:
                    step(nc.vector.reciprocal(gate1[:, 3, :], gate1[:, 7, :]))
                both, inverse = gate1[:, 0:2, :], twice(gate1[:, 3, :])
                first, rest, small = (quotient[:, k, :, :] for k in range(3))
                if part == 20:
                    step(nc.vector.tensor_tensor(first, both, inverse, ALU.mult))
                if part == 21:
                    step(nc.vector.tensor_tensor(rest, first, twice(gate1[:, 7, :]), ALU.mult))
                if part == 22:
                    step(nc.vector.tensor_tensor(small, both, rest, ALU.subtract))
                if part == 23:
                    step(nc.vector.tensor_tensor(rest, small, inverse, ALU.mult))
                if part == 24:
                    step(nc.vector.tensor_tensor(gate1[:, 4:6, :], first, rest, ALU.add))
                if part == 25:
                    step(nc.vector.tensor_tensor(
                        oh_x[:, :, :, :], oh[:, :, :, :],
                        gate1[:, 4:6, :].unsqueeze(3).to_broadcast([P, 2, QT, E]), ALU.mult))
                if part == 26:
                    step(nc.vector.tensor_tensor(some, mask, oh_x[:, 0, :, :], ALU.add))
                if part == 27:
                    step(nc.vector.tensor_tensor(
                        assigned[:, :, ds(b * QT, QT)].rearrange("p e q -> p q e"), some,
                        oh_x[:, 1, :, :], ALU.add))

            def place_rows(body, c):
                b = body.b - 1

                def after(n):
                    v.wait_ge(rank_seq, at(b, RANK_STEPS, n))

                bank = ring[:, c % 2, :]
                wait_filled(v, body, c)
                nc.vector.tensor_tensor(gate[:, 7, :, :],
                                        bank[:, 0:QT * E].rearrange("p (q e) -> p q e", e=E),
                                        list_end[:, :].unsqueeze(1).to_broadcast([P, QT, E]),
                                        ALU.add).then_inc(rank_seq, 1)
                nc.vector.tensor_copy(rows[:, :, D], token[:, :]).then_inc(rank_seq, 1)
                after(2)
                nc.vector.tensor_tensor(list_end[:, :], list_end[:, :],
                                        bank[:, QT * E:(QT + 1) * E], ALU.add)\
                    .then_inc(drained[c % 2], 1)
                nc.vector.tensor_scalar(token[:, :], token[:, :], float(N), None, ALU.add)\
                    .then_inc(rank_seq, 1)
                nc.vector.tensor_tensor(oh_x[:, :, :, :], oh[:, :, :, :],
                                        gate[:, 7, :, :].unsqueeze(1).to_broadcast([P, 2, QT, E]),
                                        ALU.mult).then_inc(rank_seq, 1)
                after(4)
                nc.vector.reduce_sum(row_f[:, :, :], oh_x[:, :, :, :], AX.X).then_inc(rank_seq, 1)
                after(5)
                nc.vector.tensor_copy(list_row[:, :, :], row_f[:, :, :]).then_inc(list_row_done, 1)

            def drain(body, u, what, c):
                kind, i, j = what
                bank = ring[:, c % 2, :]
                if kind == "h":
                    return
                if kind == "r":
                    place_rows(body, c)
                    return
                if kind == "l":
                    logits = bank[:, 0:QT * E].rearrange("p (q e) -> p q e", e=E)
                    wait_filled(v, body, c)
                    nc.vector.reduce_max(gate1[:, 2, :], logits, AX.X).then_inc(gate_seq, 1)
                    v.wait_ge(gate_seq, at(body.b - 1, GATE_STEPS, 1))
                    nc.vector.tensor_tensor(gate[:, 0, :, :], logits,
                                            gate1[:, 2, :].unsqueeze(2).to_broadcast([P, QT, E]),
                                            ALU.subtract).then_inc(drained[c % 2], 1)
                    return
                if kind == "w":
                    if i == 0:
                        v.wait_ge(biased, at(body.b, 1, 1))
                        v.wait_ge(tanh_done, 1)
                    if i == 1:
                        v.wait_ge(neg_done, at(body.b, UNITS, 0))
                    wait_filled(v, body, c)
                    part = x_sum[:, j, :]
                    nc.vector.scalar_tensor_tensor(part, bank[:, 0:D], tanh_g[:, 0:1], part,
                                                   ALU.mult, ALU.add).then_inc(drained[c % 2], 1)
                    return
                b, n = of_batch(body, what, u)
                wait_hi(v, kind, b, n)
                if kind == "q":
                    for ab in range(2):
                        for half in range(2):
                            head = slice(ab * DH, (ab + 1) * DH)
                            last = nc.vector.scalar_tensor_tensor(
                                q_l[half * DH:(half + 1) * DH, i % 2, ab, :], bank[head, :], SCALE,
                                q_h[head, i % 2, ab, :].bitcast(F32), ALU.mult, ALU.subtract)
                if kind == "k":
                    for ab in range(2):
                        head, other = slice(ab * DH, (ab + 1) * DH), slice((1 - ab) * DH, (2 - ab) * DH)
                        keys = slice(j * 512, (j + 1) * 512)
                        last = lo(k_st[other, i % 2, ab, keys], bank[head, :],
                                  k_st[head, i % 2, ab, keys])
                if kind == "v":
                    part = v_hl[:, 2 * j:2 * j + 2, 4 * i:4 * i + 4, :]
                    last = lo(part[:, :, :, DH:P], bank.rearrange("p (t h d) -> p t h d", t=2, d=DH),
                              part[:, :, :, 0:DH])
                if kind == "o":
                    toks = slice((i % 2) * 2 * P, (i % 2 + 1) * 2 * P)
                    last = lo(ot_l[:, (i // 2) % 4, toks], bank[:, 0:2 * P],
                              ot_h[:, (i // 2) % 4, toks])
                if kind == "x":
                    last = lo(xt_l[:, i, :], bank, xt_h[:, i, :])
                last.then_inc(drained[c % 2], 1)

            def low_turned(b, n, j):
                keys, toks = slice(4 * j, 4 * j + 4), slice((n % 2) * P, (n % 2 + 1) * P)
                v.wait_ge(pt_hi, at(b, 2 * UNITS, 2 * n + j + 1))
                lo(pt_l[:, (n // 2) % 2, keys, toks], turned[:, keys, :],
                   pt_h[:, (n // 2) % 2, keys, toks]).then_inc(pt_lo, 1)

            def between(body, u, gap):
                b = body.b
                if body.prev:
                    n = {(6, 4): 0, (8, 0): 1, (8, 4): 2, (9, 0): 3, (10, 0): 4, (10, 4): 5, (11, 0): 6,
                         (11, 4): 7}.get((u, gap))
                    if n is not None:
                        if n in (0, 1):
                            wait_drained(v, body, body.where[("w", 1, 2 * n + 1)])
                        layer(1, b - 1, x_sum, n)
                    n = 2 + (u - 19) * 4 + gap - 1
                    if u >= 19 and gap > 0 and n <= GATE_STEPS:
                        route(b - 1, n)
                if body.nxt:
                    n = {(12, 4): 0, (13, 0): 1, (13, 4): 2, (14, 0): 3, (15, 0): 4, (15, 4): 5,
                         (16, 0): 6, (16, 4): 7}.get((u, gap))
                    if n is not None:
                        if n == 0:
                            v.wait_ge(x_loaded, at(b + 1, 16, 16))
                        layer(0, b + 1, x_in, n)

            def run(body):
                b = body.b
                for u in range(len(body.steps)):
                    k = u % 2
                    if body is START and u in (19, 26):
                        flat = x_sum[:, :, :].rearrange("p q d -> p (q d)")
                        parts = ((wq_l, wq_h, probs[:, 0, :]), (wk_l, wk_h, probs[:, 1, :]),
                                 (wv_l, wv_h, flat))
                        for i in ((0,) if u == 19 else (1, 2)):
                            dst, hp, raw = parts[i]
                            split_raw(i, raw, dst[:, :, :].rearrange("p c n -> p (c n)"),
                                      hp[:, :, :].rearrange("p c n -> p (c n)"))
                    if body is START and u == 30:
                        v.wait_ge(tanh_done, 1)
                        nc.vector.tensor_scalar(bias_o[:, :], bias_o[:, :], tanh_g[:, 0:1], None,
                                                ALU.mult).then_inc(bias_done, 1)
                    if body is FIRST and u in (5, 8):
                        half = (u - 5) // 3
                        part = slice(half * 4, half * 4 + 4)
                        split_raw(3 + half, x_sum[:, :, :], wo_l[:, part, :], wo_h[:, part, :])
                    jobs = body.results(u)
                    for what, c in jobs[:1]:
                        drain(body, u - 1, what, c)
                    turns = body.prev if u < 3 else body.own
                    if turns:
                        low_turned(b, u - 3, 0)
                    between(body, u, 0)
                    if turns:
                        low_turned(b, u - 3, 1)
                    between(body, u, 1)
                    if body.own:
                        v.wait_ge(scores_done, at(b, UNITS, u + 1))
                        nc.vector.tensor_reduce(neg_max[:, k:k + 1],
                                                scores[:, k, :].rearrange("p (a c) -> p a c", a=2),
                                                AX.XY, ALU.max, negate=True).then_inc(neg_done, 1)
                    for what, c in jobs[1:]:
                        drain(body, u - 1, what, c)
                    between(body, u, 2)
                    between(body, u, 3)
                    if body.own if u > 0 else body.prev:
                        v.wait_ge(exp_done, at(b, UNITS, u))
                        nc.vector.reciprocal(row_rec[:, 1 - k:2 - k], row_sum[:, 1 - k:2 - k])\
                            .then_inc(rec_done, 1)
                    between(body, u, 4)
                    if body is END and u == 12:
                        for i in range(3):
                            v.wait_ge(w_first_hi, i + 1)
                            lo(w_l[0][i][:, :], w_raw[i][:, :], w_h[0][i][:, :]).then_inc(w_split, 1)

            v.wait_ge(consts, CONSTS)
            batches(v, run)

            def own(ins):
                ins.then_inc(search_seq, 1)

            v.wait_ge(drained[END.where[("r", 0, 0)] % 2],
                      at(B, RING // 2, END.where[("r", 0, 0)] // 2 + 1))
            own(nc.vector.tensor_tensor(table_f[:, 0, :], list_end[:, :], expert_row[:, :],
                                        ALU.subtract))
            v.wait_ge(search_seq, 1)
            own(nc.vector.tensor_copy(table[:, 2, :], table_f[:, 0, :]))
            own(nc.vector.tensor_scalar(table[:, 1, :], table_f[:, 0, :], float(CHUNK - 1), None,
                                        ALU.add))
            own(nc.vector.reduce_max(table_f[:, 2, 0:1], table_f[:, 0, :], AX.X))
            v.wait_ge(search_seq, 4)
            own(nc.vector.tensor_scalar(table[:, 3, :], table[:, 1, :], CHUNK.bit_length() - 1, None,
                                        ALU.arith_shift_right))
            own(nc.vector.tensor_scalar(table_f[:, 2, 1:2], table_f[:, 2, 0:1], float(CAPACITY),
                                        float(WEIGHT_BITS - 1), ALU.is_gt, ALU.mult))
            v.wait_ge(search_seq, 6)
            own(nc.vector.tensor_scalar(table[:, 0, :], table[:, 3, :], 2.0, None, ALU.max))
            own(nc.vector.tensor_scalar(table_f[:, 0, :], table[:, 3, :], 2.0, None, ALU.max))
            v.wait_ge(search_seq, 8)
            own(nc.vector.tensor_tensor_scan(table_f[:, 1, :], table_f[:, 0, :], table_f[:, 0, :], 0.0,
                                             ALU.add, ALU.bypass))
            v.wait_ge(search_seq, 9)
            nc.vector.tensor_scalar(table[:, 3, 1:2], table_f[:, 2, 1:2], 1.0, None, ALU.add)
            nc.vector.tensor_tensor(table[:, 1, :], table_f[:, 1, :], table_f[:, 0, :], ALU.subtract)
            nc.vector.tensor_copy(table[:, 3, 0:1], table_f[:, 1, E - 1:E]).then_inc(table_done, 1)

            own(nc.vector.memset(threshold[:, :], 0))
            own(nc.vector.memset(bit_f[:, :], float(1 << (WEIGHT_BITS - 1))))
            v.wait_ge(search_seq, 11)
            own(nc.vector.tensor_copy(bit[:, :], bit_f[:, :]))
            v.wait_ge(gathered, 1)
            own(nc.vector.tensor_copy(by_expert[:, :], misc[:, 0:GT]))
            v.wait_ge(search_seq, 13)
            v.wait_ge(table_done, 1)
            turns = v.value_load(table[0:1, 3, 1:2], min_val=1, max_val=WEIGHT_BITS)
            with v.Fori(0, turns) as i:
                def after(n):
                    v.wait_ge(search_bits, i * 5 + n)

                def step(ins):
                    ins.then_inc(search_bits, 1)

                v.wait_ge(search_seq, 13)
                step(nc.vector.tensor_tensor(candidate[:, :], threshold[:, :], bit[:, :],
                                             ALU.bitwise_or))
                after(1)
                nc.vector.tensor_scalar(work[:, 0, :], by_expert[:, :], candidate[:, :].bitcast(F32),
                                        0.0, ALU.is_ge, ALU.add, accum_out=counts[:, 0:1])\
                    .then_inc(counted, 1)
                v.wait_ge(summed, i + 1)
                step(nc.vector.tensor_scalar(raised[:, :], misc[:, 0:1], float(CAPACITY),
                                             bit_f[:, 0:1], ALU.is_ge, ALU.mult))
                after(2)
                step(nc.vector.tensor_tensor(threshold[:, :], threshold[:, :], raised[:, :],
                                             ALU.bitwise_or))
                step(nc.vector.tensor_scalar(bit[:, :], bit[:, :], 1, None, ALU.logical_shift_right))
                step(nc.vector.tensor_scalar(bit_f[:, :], bit_f[:, :], 0.5, None, ALU.mult))
                after(5)

            above, equal, rank, keep, room = (work[:, k, :] for k in range(5))
            lowest = threshold[:, :].bitcast(F32)
            nc.vector.tensor_scalar(above, by_expert[:, :], lowest, 0.0, ALU.is_gt, ALU.add,
                                    accum_out=counts[:, 1:2])
            nc.vector.tensor_scalar(equal, by_expert[:, :], lowest, 0.0, ALU.is_equal, ALU.add,
                                    accum_out=counts[:, 2:3]).then_inc(masked, 1)
            v.wait_ge(masked, 1)
            own(nc.vector.tensor_tensor_scan(rank, equal, equal, 0.0, ALU.add, ALU.bypass))
            v.wait_ge(ranked, 1)
            own(nc.vector.tensor_copy(counts[:, 3:4], misc[:, 0:1]))
            v.wait_ge(search_seq, 15)
            own(nc.vector.tensor_tensor(counts[:, 0:1], misc[:, 1:2], counts[:, 3:4], ALU.add))
            v.wait_ge(search_seq, 16)
            own(nc.vector.tensor_scalar(room, rank, counts[:, 0:1], float(CAPACITY),
                                        ALU.add, ALU.is_le))
            v.wait_ge(search_seq, 17)
            own(nc.vector.tensor_tensor(rank, equal, room, ALU.mult))
            v.wait_ge(search_seq, 18)
            own(nc.vector.tensor_tensor(room, rank, above, ALU.add))
            v.wait_ge(search_seq, 19)
            nc.vector.tensor_tensor(keep, by_expert[:, :], room, ALU.mult).then_inc(kept, 1)
            v.wait_ge(wsum_done, 1)
            own(nc.vector.tensor_scalar(rank, misc[:, GT:2 * GT], EPS, None, ALU.max))
            v.wait_ge(search_seq, 20)
            own(nc.vector.reciprocal(room, rank))
            v.wait_ge(search_seq, 21)
            v.wait_ge(kept, 1)
            nc.vector.scalar_tensor_tensor(by_expert[:, :], keep, tanh_g[:, 1:2], room,
                                           ALU.mult, ALU.mult).then_inc(fw_done, 1)

            def finish(n):
                v.wait_ge(weight_here, n * (16 * ST))
                v.wait_ge(ffn2_done, n * ST + 1)
                v.wait_ge(added, n * (16 * ST))
                nc.vector.tensor_scalar(y[:, 1, :], ffn2[:, 1, 0:D], y_weight[:, 1:2], None,
                                        ALU.mult).then_inc(y_done[1], 1)

            def see_tokens(loaded):
                v.wait_ge(rows_loaded, loaded)
                nc.vector.tensor_copy(next_token[:, :], e_rows[:, :, D]).then_inc(token_seen, 1)

            def low_rows(n):
                v.wait_ge(et_hi, n)
                lo(et_l[:, :, :], e_turned[:, :, :], et_h[:, :, :]).then_inc(et_lo, 1)

            def chunk(g, follows):
                for c in range(FC):
                    v.wait_ge(silu_done, g * FC + c + 1)
                    nc.vector.tensor_tensor(act_f[:, c % 2, :], ffn1[:, c % 4, 0, :], silu[:, :],
                                            ALU.mult).then_inc(act_done, 1)
                    if c == FC - 1:
                        low_rows(g + 2)
                    v.wait_ge(act_hi, g * FC + c + 1)
                    lo(act_l[:, c, :], act_f[:, c % 2, :], act_h[:, c, :]).then_inc(act_lo, 1)
                    if c == 0 and follows:
                        finish(g)
                    if c == 4:
                        v.wait_ge(added, g * (16 * ST) + 16 * ST)
                        v.wait_ge(token_seen, g + 2)
                        nc.vector.tensor_copy(y_token[:, :], next_token[:, :]).then_inc(token_copied, 1)
                        v.wait_ge(token_copied, g + 1)
                        nc.vector.tensor_scalar(y_at[:, :], next_token[:, :], e_base[:, 0:1], None,
                                                ALU.add).then_inc(token_done, 1)
                    if c == 6:
                        see_tokens(g * 16 + 32)

            nc.vector.memset(e_base[:, :], 0.0).then_inc(base_done, 1)
            see_tokens(16)
            low_rows(1)
            v.wait_ge(table_done, 1)
            with v.Fori(0, E) as e:
                chunks = v.value_load(table[0:1, 0, ds(e, 1)], min_val=2, max_val=T // CHUNK)
                before = v.value_load(table[0:1, 1, ds(e, 1)], min_val=0, max_val=MOST_CHUNKS)
                v.wait_ge(base_done, e + 1)
                chunk(v.snap(before + 0), False)
                with v.Fori(1, chunks) as j:
                    chunk(v.snap(before + j), True)
                finish(v.snap(before + chunks))
                nc.vector.tensor_scalar(e_base[:, :], e_base[:, :], float(ROWS), None, ALU.add)\
                    .then_inc(base_done, 1)


def kernel(x, ctx_1024, g_xattn, g_ffn, L0_xattn_Wq, L0_xattn_Wk, L0_xattn_Wv, L0_xattn_Wo,
           L0_xattn_bo, L0_ffn_router_weight, L0_ffn_ff_pre_act_weight, L0_ffn_gate_weight,
           L0_ffn_ff_post_act_weight):
    import numpy as np
    import concourse.bacc as bacc
    from concourse.bass_utils import run_bass_kernel_spmd

    def flat(a, rows):
        return np.ascontiguousarray(np.asarray(a)).reshape(rows, -1)

    def turned(a):
        return np.swapaxes(np.asarray(a), -1, -2)

    arrays = {
        "x": flat(x, T),
        "ctx_t": flat(turned(ctx_1024), B * D),
        "g_attn": np.asarray(g_xattn), "g_ffn": np.asarray(g_ffn),
        "wq": np.asarray(L0_xattn_Wq), "wk": np.asarray(L0_xattn_Wk), "wv": np.asarray(L0_xattn_Wv),
        "wo": np.asarray(L0_xattn_Wo), "bo": np.asarray(L0_xattn_bo),
        "rw_t": flat(turned(L0_ffn_router_weight), D),
        "w1_t": flat(turned(L0_ffn_ff_pre_act_weight), E * D),
        "wg_t": flat(turned(L0_ffn_gate_weight), E * D),
        "w2_t": flat(turned(L0_ffn_ff_post_act_weight), E * FF),
    }
    nc = bacc.Bacc("TRN2", target_bir_lowering=False, num_devices=1)
    args = {name: nc.dram_tensor(name, a.shape, mybir.dt.from_np(a.dtype), kind="ExternalInput").ap()
            for name, a in arrays.items()}
    out = nc.dram_tensor("out", (ROWS, D), F32, kind="ExternalOutput").ap()
    build(nc, out=out, **args)
    result = run_bass_kernel_spmd(nc, [arrays], core_ids=[0])
    return result.results[0]["out"][:T].reshape(B, N, D)
```
